# Optimizing a Trainium2 kernel written in Bass

```python
import numpy as np
import jax
import jax.numpy as jnp

def _softmax(x, axis=-1):
    return jax.nn.softmax(x, axis=axis)

def _gelu(x):
    return jax.nn.gelu(x, approximate=True)

def _silu(x):
    return jax.nn.silu(x)

def _sigmoid(x):
    return jax.nn.sigmoid(x)

def _layernorm(x, axis=-1, eps=1e-05):
    m = jnp.mean(x, axis=axis, keepdims=True)
    v = jnp.var(x, axis=axis, keepdims=True)
    return (x - m) / jnp.sqrt(v + eps)

def _scatter_add(tgt, idx, src, axis=0):
    return tgt.at[idx].add(src)

def _segment_sum(src, seg, n):
    return jax.ops.segment_sum(src, seg, n)
kernel_name = 'mk_macaron_d1_jaxref_r8_7cf0ea'

def setup_inputs(seed: int=0):
    np.random.seed(seed)
    _w = jnp.asarray

    def _L0_attn_setup():
        import jax, jax.numpy as jnp
        import numpy as np
        DIM = 256
        QK_DIM = 128
        HIDDEN = int(2.0 * DIM)
        key = jax.random.key(seed)
        ks = jax.random.split(key, 8)
        s = lambda fan_in: 1.0 / np.sqrt(fan_in)
        return {'x': jax.random.normal(ks[0], (4, 256, DIM), dtype=jnp.float32), 'W_hidden': jax.random.normal(ks[1], (DIM, HIDDEN * 2), dtype=jnp.float32) * s(DIM), 'b_hidden': jnp.zeros((HIDDEN * 2,), dtype=jnp.float32), 'W_qk': jax.random.normal(ks[2], (DIM, QK_DIM), dtype=jnp.float32) * s(DIM), 'b_qk': jnp.zeros((QK_DIM,), dtype=jnp.float32), 'gamma_q': jnp.ones((QK_DIM,), dtype=jnp.float32), 'beta_q': jnp.zeros((QK_DIM,), dtype=jnp.float32), 'gamma_k': jnp.ones((QK_DIM,), dtype=jnp.float32), 'beta_k': jnp.zeros((QK_DIM,), dtype=jnp.float32), 'W_out': jax.random.normal(ks[3], (HIDDEN, DIM), dtype=jnp.float32) * s(HIDDEN), 'b_out': jnp.zeros((DIM,), dtype=jnp.float32)}
    _L0_attn_in = _L0_attn_setup()

    def _L0_ffn_setup():
        import jax, jax.numpy as jnp
        import numpy as np
        import math
        GOLDEN_CENTER = 1.0 / math.e
        GOLDEN_LOWER = 0.5 - math.log(4.0 / 3.0)
        GOLDEN_UPPER = 0.5
        B, T, D = (4, 128, 256)
        E = 8
        F = 1024 // (E // 2)
        R = 64
        NL = 2

        def _router_weights(x, Wr, temperature):
            logits = jnp.einsum('btd,de->bte', x, Wr)
            inhibition = jax.nn.sigmoid(logits / temperature)
            in_zone = (inhibition >= GOLDEN_LOWER) & (inhibition <= GOLDEN_UPPER)
            distance = jnp.abs(inhibition - GOLDEN_CENTER)
            w = jnp.exp(-distance / 0.1) * in_zone.astype(x.dtype)
            wsum = w.sum(axis=-1, keepdims=True)
            no_expert = wsum < 1e-08
            fb = jnp.exp(-distance / 0.3)
            _, top2 = jax.lax.top_k(fb, 2)
            fb_mask = jax.nn.one_hot(top2, E, dtype=x.dtype).sum(axis=-2)
            fb_w = fb * fb_mask
            fb_w = fb_w / jnp.clip(fb_w.sum(axis=-1, keepdims=True), 1e-08)
            w = jnp.where(no_expert, fb_w, w)
            return w / jnp.clip(w.sum(axis=-1, keepdims=True), 1e-08)
        key = jax.random.key(seed)
        ks = jax.random.split(key, 13)
        s = 0.02
        x = jax.random.normal(ks[0], (B, T, D), dtype=jnp.float32)
        Wg = jax.random.normal(ks[1], (E, D, F), dtype=jnp.float32) * s
        Wu = jax.random.normal(ks[2], (E, D, F), dtype=jnp.float32) * s
        Wd = jax.random.normal(ks[3], (E, F, D), dtype=jnp.float32) * s
        Ga = jax.random.normal(ks[4], (NL, D, R), dtype=jnp.float32) * s
        Gb = jax.random.normal(ks[5], (NL, R, F), dtype=jnp.float32) * s
        Ua = jax.random.normal(ks[6], (NL, D, R), dtype=jnp.float32) * s
        Ub = jax.random.normal(ks[7], (NL, R, F), dtype=jnp.float32) * s
        Da = jax.random.normal(ks[8], (NL, F, R), dtype=jnp.float32) * s
        Db = jax.random.normal(ks[9], (NL, R, D), dtype=jnp.float32) * s
        Wr = jax.random.normal(ks[10], (D, E), dtype=jnp.float32) * s
        temperature = jnp.ones((1,), dtype=jnp.float32)
        return {'x': x, 'Wg': Wg, 'Wu': Wu, 'Wd': Wd, 'Ga': Ga, 'Gb': Gb, 'Ua': Ua, 'Ub': Ub, 'Da': Da, 'Db': Db, 'Wr': Wr, 'temperature': temperature}
    _L0_ffn_in = _L0_ffn_setup()
    _d = {'L0_attn_x': _L0_attn_in['x'], 'L0_attn_W_hidden': _L0_attn_in['W_hidden'], 'L0_attn_b_hidden': _L0_attn_in['b_hidden'], 'L0_attn_W_qk': _L0_attn_in['W_qk'], 'L0_attn_b_qk': _L0_attn_in['b_qk'], 'L0_attn_gamma_q': _L0_attn_in['gamma_q'], 'L0_attn_beta_q': _L0_attn_in['beta_q'], 'L0_attn_gamma_k': _L0_attn_in['gamma_k'], 'L0_attn_beta_k': _L0_attn_in['beta_k'], 'L0_attn_W_out': _L0_attn_in['W_out'], 'L0_attn_b_out': _L0_attn_in['b_out'], 'L0_ffn_Wg': _L0_ffn_in['Wg'], 'L0_ffn_Wu': _L0_ffn_in['Wu'], 'L0_ffn_Wd': _L0_ffn_in['Wd'], 'L0_ffn_Ga': _L0_ffn_in['Ga'], 'L0_ffn_Gb': _L0_ffn_in['Gb'], 'L0_ffn_Ua': _L0_ffn_in['Ua'], 'L0_ffn_Ub': _L0_ffn_in['Ub'], 'L0_ffn_Da': _L0_ffn_in['Da'], 'L0_ffn_Db': _L0_ffn_in['Db'], 'L0_ffn_Wr': _L0_ffn_in['Wr'], 'L0_ffn_temperature': _L0_ffn_in['temperature']}
    _x0 = _d['L0_attn_x']
    _d['L0_attn_x'] = jax.random.normal(jax.random.fold_in(jax.random.key(seed), 1), (8, 256, 256), dtype=_x0.dtype)
    del _x0
    return _d

def reference(L0_attn_x, L0_attn_W_hidden, L0_attn_b_hidden, L0_attn_W_qk, L0_attn_b_qk, L0_attn_gamma_q, L0_attn_beta_q, L0_attn_gamma_k, L0_attn_beta_k, L0_attn_W_out, L0_attn_b_out, L0_ffn_Wg, L0_ffn_Wu, L0_ffn_Wd, L0_ffn_Ga, L0_ffn_Gb, L0_ffn_Ua, L0_ffn_Ub, L0_ffn_Da, L0_ffn_Db, L0_ffn_Wr, L0_ffn_temperature):

    def _L0_attn_ref(x, W_hidden, b_hidden, W_qk, b_qk, gamma_q, beta_q, gamma_k, beta_k, W_out, b_out):
        import jax, jax.numpy as jnp
        import numpy as np
        DIM = 256
        QK_DIM = 128
        HIDDEN = int(2.0 * DIM)
        seq_len = x.shape[-2]
        hidden = jax.nn.silu(jnp.einsum('bnd,dh->bnh', x, W_hidden) + b_hidden)
        v, gate = jnp.split(hidden, 2, axis=-1)
        qk = jax.nn.silu(jnp.einsum('bnd,de->bne', x, W_qk) + b_qk)
        q = qk * gamma_q + beta_q
        k = qk * gamma_k + beta_k
        sim = jnp.einsum('bie,bje->bij', q, k) / seq_len
        attn = jnp.square(jax.nn.relu(sim))
        out = jnp.einsum('bij,bjh->bih', attn, v) * gate
        out = jnp.einsum('bih,hd->bid', out, W_out) + b_out
        return out + x

    def _L0_ffn_ref(x, Wg, Wu, Wd, Ga, Gb, Ua, Ub, Da, Db, Wr, temperature):
        import jax, jax.numpy as jnp
        import numpy as np
        import math
        GOLDEN_CENTER = 1.0 / math.e
        GOLDEN_LOWER = 0.5 - math.log(4.0 / 3.0)
        GOLDEN_UPPER = 0.5
        B, T, D = (4, 128, 256)
        E = 8
        F = 1024 // (E // 2)
        R = 64
        NL = 2

        def _router_weights(x, Wr, temperature):
            logits = jnp.einsum('btd,de->bte', x, Wr)
            inhibition = jax.nn.sigmoid(logits / temperature)
            in_zone = (inhibition >= GOLDEN_LOWER) & (inhibition <= GOLDEN_UPPER)
            distance = jnp.abs(inhibition - GOLDEN_CENTER)
            w = jnp.exp(-distance / 0.1) * in_zone.astype(x.dtype)
            wsum = w.sum(axis=-1, keepdims=True)
            no_expert = wsum < 1e-08
            fb = jnp.exp(-distance / 0.3)
            _, top2 = jax.lax.top_k(fb, 2)
            fb_mask = jax.nn.one_hot(top2, E, dtype=x.dtype).sum(axis=-2)
            fb_w = fb * fb_mask
            fb_w = fb_w / jnp.clip(fb_w.sum(axis=-1, keepdims=True), 1e-08)
            w = jnp.where(no_expert, fb_w, w)
            return w / jnp.clip(w.sum(axis=-1, keepdims=True), 1e-08)
        weights = _router_weights(x, Wr, temperature)
        gate = jnp.einsum('btd,edf->ebtf', x, Wg)
        up = jnp.einsum('btd,edf->ebtf', x, Wu)
        gate = gate.at[:NL].add(jnp.einsum('btd,edr,erf->ebtf', x, Ga, Gb))
        up = up.at[:NL].add(jnp.einsum('btd,edr,erf->ebtf', x, Ua, Ub))
        mid = jax.nn.silu(gate) * up
        out = jnp.einsum('ebtf,efd->ebtd', mid, Wd)
        out = out.at[:NL].add(jnp.einsum('ebtf,efr,erd->ebtd', mid[:NL], Da, Db))
        return jnp.einsum('bte,ebtd->btd', weights, out)
    x = L0_attn_x
    x = x + 0.5 * _L0_ffn_ref(_layernorm(x, axis=-1), L0_ffn_Wg, L0_ffn_Wu, L0_ffn_Wd, L0_ffn_Ga, L0_ffn_Gb, L0_ffn_Ua, L0_ffn_Ub, L0_ffn_Da, L0_ffn_Db, L0_ffn_Wr, L0_ffn_temperature)
    x = x + _L0_attn_ref(_layernorm(x, axis=-1), L0_attn_W_hidden, L0_attn_b_hidden, L0_attn_W_qk, L0_attn_b_qk, L0_attn_gamma_q, L0_attn_beta_q, L0_attn_gamma_k, L0_attn_beta_k, L0_attn_W_out, L0_attn_b_out)
    x = x + 0.5 * _L0_ffn_ref(_layernorm(x, axis=-1), L0_ffn_Wg, L0_ffn_Wu, L0_ffn_Wd, L0_ffn_Ga, L0_ffn_Gb, L0_ffn_Ua, L0_ffn_Ub, L0_ffn_Da, L0_ffn_Db, L0_ffn_Wr, L0_ffn_temperature)
    return x

_drawn_inputs = setup_inputs


def setup_inputs(seed=0):
    import zlib

    import numpy as np

    out = dict(_drawn_inputs(seed))
    spreads = {'L0_attn_b_hidden': (0.0, 0.8),
     'L0_attn_b_qk': (0.0, 0.8),
     'L0_attn_gamma_q': (1.0, 0.6),
     'L0_attn_beta_q': (0.0, 2.0),
     'L0_attn_gamma_k': (1.0, 0.6),
     'L0_attn_beta_k': (0.0, 0.8),
     'L0_attn_b_out': (0.0, 0.8)}
    factors = {'L0_attn_W_qk': 5.452,
     'L0_ffn_Wg': 7.952,
     'L0_ffn_Wu': 7.841,
     'L0_ffn_Wd': 7.844,
     'L0_ffn_Ga': 8.0,
     'L0_ffn_Gb': 8.0,
     'L0_ffn_Ua': 8.0,
     'L0_ffn_Ub': 8.0,
     'L0_ffn_Da': 8.0,
     'L0_ffn_Db': 8.0,
     'L0_ffn_Wr': 8.0}
    for name, (base, spread) in spreads.items():
        noise = np.random.default_rng([zlib.crc32(name.encode()), seed]).standard_normal(out[name].shape)
        drawn = base * np.exp(spread * noise) if base else spread * noise
        out[name] = jnp.asarray(drawn.astype(out[name].dtype))
    for name, factor in factors.items():
        out[name] = (out[name] * factor).astype(out[name].dtype)
    return out
```

```python
import math
from contextlib import ExitStack

import concourse.bass as bass
from concourse import mybir
from concourse.alu_op_type import AluOpType as ALU

F32 = mybir.dt.float32
F32R = mybir.dt.float32r
I32 = mybir.dt.int32
ACT = mybir.ActivationFunctionType
AX = mybir.AxisListType

P = 128
SEQS, SEQ, D = 8, 256, 256
TOKENS = SEQS * SEQ
CHUNK = 512
CHUNKS = TOKENS // CHUNK
TPC = CHUNK // P
TILES = TOKENS // P
KD = D // P
E, F, NL, RANK = 8, 256, 2, 64
KF = F // P
HID, QK = 512, 128
HT = HID // P
BPC = CHUNK // SEQ
UNITS = E * CHUNKS
EPS = 1e-5
SLOT_EXPERT = [(s + NL) % E for s in range(E)]

GOLDEN_CENTER = 1.0 / math.e
GOLDEN_LOWER = 0.5 - math.log(4.0 / 3.0)
GOLDEN_UPPER = 0.5


def build(nc, x_in, w_hidden, b_hidden, w_qk, b_qk, gamma_q, beta_q, gamma_k, beta_k, w_out, b_out,
          wg, wu, wd, ga, gb, ua, ub, da, db, wr, temperature, out):
    ctx = ExitStack()
    with ctx:
        def sb(name, shape, dt=F32):
            return ctx.enter_context(nc.sbuf_tensor(name, shape, dt))

        def ps(name):
            return ctx.enter_context(nc.psum_tensor(name, [P, 512], F32))

        def sem(name):
            return ctx.enter_context(nc.semaphore(name))

        x_res = sb("x_res", [P, TILES, D])
        xn = sb("xn", [P, TPC, D])
        xt_h = sb("xt_h", [P, CHUNKS + 1, 2 * CHUNK], F32R)
        xt_l = sb("xt_l", [P, CHUNKS + 1, 2 * CHUNK], F32R)
        mid_h = sb("mid_h", [P, 2, KF, CHUNK], F32R)
        mid_l = sb("mid_l", [P, 2, KF, CHUNK], F32R)
        w_raw_gu = sb("w_raw_gu", [P, E, KD, 2 * F])
        w_raw_d = sb("w_raw_d", [P, E, KF, D])
        w_gu_h = sb("w_gu_h", [P, 2, KD, 2 * F], F32R)
        w_gu_l = sb("w_gu_l", [P, 2, KD, 2 * F], F32R)
        w_d_h = sb("w_d_h", [P, 2, KF, D], F32R)
        w_d_l = sb("w_d_l", [P, 2, KF, D], F32R)
        w_hid_h = sb("w_hid_h", [P, KD, 2 * HID], F32R)
        w_hid_l = sb("w_hid_l", [P, KD, 2 * HID], F32R)
        w_out_h = sb("w_out_h", [P, HT, D], F32R)
        w_out_l = sb("w_out_l", [P, HT, D], F32R)
        w_qk_h = sb("w_qk_h", [P, KD, QK], F32R)
        w_qk_l = sb("w_qk_l", [P, KD, QK], F32R)
        w_qk_raw = sb("w_qk_raw", [P, KD, QK])
        gate_t = sb("gate_t", [P, HT, CHUNK])
        w_hid_raw = gate_t[:, :, :].rearrange("p h c -> p (h c)").rearrange("p (k n) -> p k n", k=KD)
        work = sb("work", [P, 6, CHUNK])
        w_out_raw = work[:, 4:6, :].rearrange("p a b -> p (a b)").rearrange("p (h n) -> p h n", h=HT)
        ident = sb("ident", [P, P])
        bias_v = sb("bias_v", [P, HID])
        bias_o = sb("bias_o", [P, D])
        bias_g = sb("bias_g", [P, HT])
        vecs = sb("vecs", [P, 5])
        spare = gate_t[:, :, :].rearrange("p h c -> p (h c)")
        lora_a = work[:, 4:6, :].rearrange("p a b -> p (a b)")[:, 0:3 * NL * 2 * RANK].rearrange(
            "p (i e k r) -> p i e k r", i=3, e=NL, k=2)
        lora_b = spare[0:RANK, 0:3 * NL * F].rearrange("p (i e f) -> p i e f", i=3, e=NL)
        lora_t = spare[0:RANK, 3 * NL * F:3 * NL * F + 4 * P].rearrange("p (n k f) -> p n k f", n=2, k=2)
        wr_raw = sb("wr_raw", [P, KD, E])
        wr_hl = sb("wr_hl", [P, KD, 2, E], F32R)
        temp = sb("temp", [P, 1])
        half_inv_temp = sb("half_inv_temp", [P, 1])
        tie_key = sb("tie_key", [P, TPC, E])
        bn6 = sb("bn6", [P, TPC, 6])
        mv = sb("mv", [P, TPC, 2])
        nw = sb("nw", [P, 4, TPC])
        route = sb("route", [P, TILES, E])
        rt = sb("rt", [P, 12, TPC, E])
        rs = sb("rs", [P, 4, TPC])

        bank_g = [ps("bank_g0"), ps("bank_g1")]
        bank_u = [ps("bank_u0"), ps("bank_u1")]
        bank_d = [ps("bank_d0"), ps("bank_d1")]
        bank_t = [ps("bank_t0"), ps("bank_t1")]

        x_loaded = [sem(f"x_loaded{c}") for c in range(CHUNKS)]
        slot_loaded = [sem("slot0_loaded"), sem("slot1_loaded"), sem("slots_rest_loaded")]
        router_loaded = sem("router_loaded")
        lora_loaded = sem("lora_loaded")
        attn_loaded = sem("attn_loaded")
        out_stored = sem("out_stored")
        ident_ready = sem("ident_ready")
        pool_step = sem("pool_step")
        dve_step = sem("dve_step")
        router_w_ready = sem("router_w_ready")
        xn_ready = sem("xn_ready")
        xt_psum = sem("xt_psum")
        xh_ready = sem("xh_ready")
        xl_ready = sem("xl_ready")
        logits_psum = sem("logits_psum")
        logits_read = sem("logits_read")
        tanh_z = sem("tanh_z")
        dist_ready = sem("dist_ready")
        tanh_d = sem("tanh_d")
        wh_ready = sem("wh_ready")
        wl_ready = sem("wl_ready")
        gu_psum = sem("gu_psum")
        silu_ready = sem("silu_ready")
        mid_ready = sem("mid_ready")
        mh_ready = sem("mh_ready")
        ml_ready = sem("ml_ready")
        down_psum = sem("down_psum")
        added = sem("added")
        lora_tr_psum = sem("lora_tr_psum")
        lora_tr = sem("lora_tr")
        lora_psum = sem("lora_psum")
        lora_added = sem("lora_added")
        attn_wh_ready = sem("attn_wh_ready")
        attn_wl_ready = sem("attn_wl_ready")
        qk_psum = sem("qk_psum")
        qk_ready = sem("qk_ready")
        q_k_ready = sem("q_k_ready")
        qkh_ready = sem("qkh_ready")
        qkl_ready = sem("qkl_ready")
        v_psum = sem("v_psum")
        vb_ready = sem("vb_ready")
        v_ready = sem("v_ready")
        vh_ready = sem("vh_ready")
        vl_ready = sem("vl_ready")
        gate_psum = sem("gate_psum")
        gate_ready = sem("gate_ready")
        sim_psum = sem("sim_psum")
        relu_ready = sem("relu_ready")
        sq_ready = sem("sq_ready")
        ah_ready = sem("ah_ready")
        al_ready = sem("al_ready")
        av_psum = sem("av_psum")
        og_ready = sem("og_ready")
        oh_ready = sem("oh_ready")
        ol_ready = sem("ol_ready")
        down_psum_attn = sem("down_psum_attn")
        resid_ready = sem("resid_ready")

        L_ADDED = [0, 2 * UNITS + 2 * CHUNKS]
        A_ADDED = 2 * UNITS

        def n_uf(layer, u, f):
            return u * KF + (layer * UNITS * KF + f + 1)

        def n_down(layer, u, b):
            return u * 2 + (layer * UNITS * 2 + b + 1)

        def n_added(layer, u, b):
            return u * 2 + (L_ADDED[layer] + b + 1)

        def g_of(layer, c):
            return 2 * CHUNKS * layer + c

        def w_col(ap, s):
            return ap[:, bass.ds(s, 1)]

        def v_region(t, n=HID):
            return 1 + t // 2, (t % 2) * HID

        def gated_region(h, b):
            return 3 + b, h * SEQ

        block = ctx.enter_context(nc.Block())

        x_tiles = x_in.rearrange("b (h p) d -> p (b h) d", p=P)
        out_tiles = out.rearrange("b (h p) d -> p (b h) d", p=P)

        @block.sync
        def _(sp):
            def load_slot(s, done):
                e = SLOT_EXPERT[s]
                sp.dma_start(w_raw_gu[:, s, :, 0:F], wg[e].rearrange("(k p) f -> p k f", p=P)).then_inc(done, 16)
                sp.dma_start(w_raw_gu[:, s, :, F:2 * F], wu[e].rearrange("(k p) f -> p k f", p=P)).then_inc(done, 16)
                sp.dma_start(w_raw_d[:, s], wd[e].rearrange("(k p) f -> p k f", p=P)).then_inc(done, 16)

            load_slot(0, slot_loaded[0])
            sp.dma_start(wr_raw[:, :, 0:E - NL], wr[:, NL:E].rearrange("(k p) e -> p k e", p=P)).then_inc(router_loaded, 16)
            sp.dma_start(wr_raw[:, :, E - NL:E], wr[:, 0:NL].rearrange("(k p) e -> p k e", p=P)).then_inc(router_loaded, 16)
            sp.dma_start(temp[:, :], temperature.partition_broadcast(P)).then_inc(router_loaded, 16)
            load_slot(1, slot_loaded[1])
            for i, a in enumerate((ga, ua, da)):
                for e in range(NL):
                    sp.dma_start(lora_a[:, i, e], a[e].rearrange("(k p) r -> p k r", p=P)).then_inc(lora_loaded, 16)
            for i, b in enumerate((gb, ub, db)):
                for e in range(NL):
                    sp.dma_start(lora_b[:, i, e], b[e]).then_inc(lora_loaded, 16)
            for s in range(2, E):
                load_slot(s, slot_loaded[2])
            sp.wait_ge(lora_added, 3 * NL)
            sp.dma_start(w_hid_raw, w_hidden.rearrange("(k p) n -> p k n", p=P)).then_inc(attn_loaded, 16)
            sp.dma_start(w_out_raw, w_out.rearrange("(h p) n -> p h n", p=P)).then_inc(attn_loaded, 16)
            sp.dma_start(w_qk_raw[:, :, :], w_qk.rearrange("(k p) n -> p k n", p=P)).then_inc(attn_loaded, 16)
            for i, v in enumerate((b_qk, gamma_q, beta_q, gamma_k, beta_k)):
                sp.dma_start(vecs[:, i:i + 1], v.rearrange("(p o) -> p o", o=1)).then_inc(attn_loaded, 16)
            for h in range(HT):
                sp.dma_start(bias_g[:, h:h + 1], b_hidden[HID + h * P:HID + (h + 1) * P].rearrange("(p o) -> p o", o=1)).then_inc(attn_loaded, 16)
            sp.dma_start(bias_v[:, :], b_hidden[0:HID].partition_broadcast(P)).then_inc(attn_loaded, 16)
            sp.dma_start(bias_o[:, :], b_out.partition_broadcast(P)).then_inc(attn_loaded, 16)
            for c in range(CHUNKS):
                sp.wait_ge(added, n_added(1, UNITS - CHUNKS + c, 1))
                sp.dma_start(out_tiles[:, c * TPC:(c + 1) * TPC], x_res[:, c * TPC:(c + 1) * TPC]).then_inc(out_stored, 16)
            sp.wait_ge(out_stored, 16 * CHUNKS)

        N_ATTN_LOADS = 16 * (3 + 5 + HT + 2)
        N_LORA_LOADS = 16 * 6 * NL
        N_SLOT_LOADS = 16 * 3

        @block.tensor
        def _(pe):
            def transposes(g, first=False):
                pe.wait_ge(xn_ready, g + 1)
                if first:
                    pe.wait_ge(ident_ready, 2)
                for k in range(KD):
                    for t in range(TPC):
                        last = nc.tensor.transpose(bank_t[k][:, t * P:(t + 1) * P], xn[:, t, k * P:(k + 1) * P], ident[:, :])
                last.then_inc(xt_psum, 1)

            def logits(layer, c):
                g = g_of(layer, c)
                pe.wait_ge(xh_ready, g + 1)
                pe.wait_ge(xl_ready, g + 1)
                if layer == 0 and c == 0:
                    pe.wait_ge(router_w_ready, 1)
                for t in range(TPC):
                    for i, (xt, k) in enumerate([(xt, k) for k in range(KD) for xt in (xt_h, xt_l)]):
                        last = nc.tensor.matmul(bank_t[0][:, t * 2 * E:(t + 1) * 2 * E],
                                                xt[:, c, k * CHUNK + t * P:k * CHUNK + (t + 1) * P],
                                                wr_hl[:, k].rearrange("p a e -> p (a e)"),
                                                start=(i == 0), stop=(i == 2 * KD - 1))
                last.then_inc(logits_psum, 1)

            def gate_up(layer, u, par, c, f):
                if c == 0 and f == 0:
                    s = 0 if isinstance(u, int) and u == 0 else None
                    pe.wait_ge(wh_ready, (u // CHUNKS if isinstance(u, int) else slot_of[0]) + (layer * E + 1))
                    pe.wait_ge(wl_ready, (u // CHUNKS if isinstance(u, int) else slot_of[0]) + (layer * E + 1))
                if isinstance(u, int) and u < CHUNKS and f == 0:
                    pe.wait_ge(xh_ready, g_of(layer, c) + 1)
                    pe.wait_ge(xl_ready, g_of(layer, c) + 1)
                if not (layer == 0 and isinstance(u, int) and u == 0):
                    pe.wait_ge(mid_ready, n_uf(layer, u, f) - KF)
                for bank, col in ((bank_g[f], f * P), (bank_u[f], F + f * P)):
                    for k in range(KD):
                        xh = xt_h[:, c, k * CHUNK:(k + 1) * CHUNK]
                        xl = xt_l[:, c, k * CHUNK:(k + 1) * CHUNK]
                        wh = w_gu_h[:, par, k, col:col + P]
                        wl = w_gu_l[:, par, k, col:col + P]
                        nc.tensor.matmul(bank[:, :], wh, xh, start=(k == 0), stop=False)
                        nc.tensor.matmul(bank[:, :], wh, xl, start=False, stop=False)
                        last = nc.tensor.matmul(bank[:, :], wl, xh, start=False, stop=(k == KD - 1))
                last.then_inc(gu_psum, 1)

            def down(layer, u, par, c, first=False):
                pe.wait_ge(mh_ready, n_uf(layer, u, KF - 1))
                pe.wait_ge(ml_ready, n_uf(layer, u, KF - 1))
                m = c % 2
                for b in range(2):
                    if not first:
                        pe.wait_ge(added, n_added(layer, u, b) - 2)
                    for t in (2 * b, 2 * b + 1):
                        o = bank_d[b][:, (t % 2) * D:(t % 2 + 1) * D]
                        for k in range(KF):
                            mh = mid_h[:, m, k, t * P:(t + 1) * P]
                            ml = mid_l[:, m, k, t * P:(t + 1) * P]
                            nc.tensor.matmul(o, mh, w_d_h[:, par, k, :], start=(k == 0), stop=False)
                            nc.tensor.matmul(o, mh, w_d_l[:, par, k, :], start=False, stop=False)
                            last = nc.tensor.matmul(o, ml, w_d_h[:, par, k, :], start=False, stop=(k == KF - 1))
                    last.then_inc(down_psum, 1)

            def low_rank():
                pe.wait_ge(lora_loaded, N_LORA_LOADS)
                for n, (i, e) in enumerate([(i, e) for i in range(3) for e in range(NL)]):
                    if n == 0:
                        pe.wait_ge(logits_read, CHUNKS)
                    else:
                        pe.wait_ge(lora_tr, n)
                    for k in range(2):
                        last = nc.tensor.transpose(bank_t[0][0:RANK, k * P:(k + 1) * P], lora_a[:, i, e, k, :], ident[:, :])
                    last.then_inc(lora_tr_psum, 1)
                    pe.wait_ge(lora_tr, n + 1)
                    if n > 0:
                        pe.wait_ge(lora_added, n)
                    for k in range(2):
                        last = nc.tensor.matmul(bank_t[1][:, k * F:(k + 1) * F], lora_t[:, n % 2, k, :], lora_b[:, i, e, :],
                                                start=True, stop=True)
                    last.then_inc(lora_psum, 1)

            slot_of = [None]

            def ffn(layer):
                if layer == 0:
                    transposes(0, first=True)
                for u in range(2 * CHUNKS):
                    c, par = u % CHUNKS, u // CHUNKS
                    gate_up(layer, u, par, c, 0)
                    if u < CHUNKS:
                        logits(layer, c)
                    gate_up(layer, u, par, c, 1)
                    if u + 1 < CHUNKS:
                        pe.wait_ge(logits_read, layer * CHUNKS + c + 1)
                        transposes(g_of(layer, u + 1))
                    if u > 0:
                        down(layer, u - 1, (u - 1) // CHUNKS, (u - 1) % CHUNKS, first=(layer == 0 and u == 1))
                    if u == CHUNKS and layer == 0:
                        low_rank()
                with pe.Fori(1, E // 2) as pair:
                    for j in range(2 * CHUNKS):
                        c, par = j % CHUNKS, j // CHUNKS
                        slot_of[0] = pair * 2 + par
                        u = pair * (2 * CHUNKS) + j
                        gate_up(layer, u, par, c, 0)
                        gate_up(layer, u, par, c, 1)
                        jd = (j - 1) % (2 * CHUNKS)
                        down(layer, pair * (2 * CHUNKS) + (j - 1), jd // CHUNKS, jd % CHUNKS)
                down(layer, UNITS - 1, 1, CHUNKS - 1)

            def project(bank, lh, ll, rh, rl, ks):
                for k in range(ks):
                    nc.tensor.matmul(bank, lh(k), rh(k), start=(k == 0), stop=False)
                    nc.tensor.matmul(bank, lh(k), rl(k), start=False, stop=False)
                    last = nc.tensor.matmul(bank, ll(k), rh(k), start=False, stop=(k == ks - 1))
                return last

            def attention():
                pe.wait_ge(attn_wh_ready, 1)
                pe.wait_ge(attn_wl_ready, 1)
                transposes(CHUNKS)
                with pe.Fori(0, CHUNKS) as c:
                    def xh(k):
                        return xt_h[:, 0, k * CHUNK:(k + 1) * CHUNK]

                    def xl(k):
                        return xt_l[:, 0, k * CHUNK:(k + 1) * CHUNK]

                    pe.wait_ge(xh_ready, c + (CHUNKS + 1))
                    pe.wait_ge(xl_ready, c + (CHUNKS + 1))
                    project(bank_g[0][:, :], lambda k: w_qk_h[:, k, :], lambda k: w_qk_l[:, k, :], xh, xl, KD).then_inc(qk_psum, 1)
                    v_bank = [bank_u[0], bank_g[1], bank_u[1], bank_g[0]]
                    for t in range(TPC):
                        if t == 3:
                            pe.wait_ge(qk_ready, c + 1)
                        project(v_bank[t][:, :],
                                lambda k: xt_h[:, 0, k * CHUNK + t * P:k * CHUNK + (t + 1) * P],
                                lambda k: xt_l[:, 0, k * CHUNK + t * P:k * CHUNK + (t + 1) * P],
                                lambda k: w_hid_h[:, k, 0:HID], lambda k: w_hid_l[:, k, 0:HID], KD).then_inc(v_psum, 1)

                    def gate(h):
                        pe.wait_ge(vb_ready, c * TPC + (h + 1))
                        col = HID + h * P
                        project(v_bank[h][:, :], lambda k: w_hid_h[:, k, col:col + P],
                                lambda k: w_hid_l[:, k, col:col + P], xh, xl, KD).then_inc(gate_psum, 1)

                    def similarity(b):
                        for j in range(2):
                            o = bank_t[b][:, j * SEQ:(j + 1) * SEQ]
                            ks = slice(b * SEQ + j * P, b * SEQ + (j + 1) * P)
                            qs = slice(b * SEQ, (b + 1) * SEQ)
                            last = project(o, lambda k: mid_h[:, 0, 1, ks], lambda k: mid_l[:, 0, 1, ks],
                                           lambda k: mid_h[:, 0, 0, qs], lambda k: mid_l[:, 0, 0, qs], 1)
                        last.then_inc(sim_psum, 1)

                    gate(0)
                    gate(1)
                    pe.wait_ge(qkh_ready, c * 2 + 2)
                    pe.wait_ge(qkl_ready, c * 2 + 2)
                    similarity(0)
                    similarity(1)
                    gate(2)
                    gate(3)
                    pe.wait_ge(relu_ready, c * 2 + 2)
                    transposes(c + (CHUNKS + 1))
                    av_bank = [bank_u[0], bank_g[1], bank_u[1], bank_g[0]]
                    pe.wait_ge(vh_ready, c * TPC + TPC)
                    pe.wait_ge(vl_ready, c * TPC + TPC)
                    for b in range(BPC):
                        pe.wait_ge(ah_ready, c * 2 + (b + 1))
                        pe.wait_ge(al_ready, c * 2 + (b + 1))
                        for hp in range(2):
                            pe.wait_ge(gate_ready, c * HT + (2 * b + hp + 1))
                            for h in (2 * hp, 2 * hp + 1):
                                def v_part(buf, k):
                                    r, o = v_region(2 * b + k)
                                    return buf[:, r, o + h * P:o + (h + 1) * P]

                                last = project(av_bank[2 * b + hp][:, (h % 2) * SEQ:(h % 2 + 1) * SEQ],
                                               lambda k: v_part(xt_h, k), lambda k: v_part(xt_l, k),
                                               lambda k: mid_h[:, 1, b, k * SEQ:(k + 1) * SEQ],
                                               lambda k: mid_l[:, 1, b, k * SEQ:(k + 1) * SEQ], 2)
                            last.then_inc(av_psum, 1)
                    for b in range(BPC):
                        pe.wait_ge(oh_ready, c * 4 + (2 * b + 2))
                        pe.wait_ge(ol_ready, c * 4 + (2 * b + 2))
                        pe.wait_ge(added, c * 2 + (A_ADDED + b - 1))
                        for t in range(2):
                            def o_part(buf, k):
                                r, o = gated_region(k, b)
                                return buf[:, r, o + t * P:o + (t + 1) * P]

                            last = project(bank_d[b][:, t * D:(t + 1) * D],
                                           lambda k: o_part(xt_h, k), lambda k: o_part(xt_l, k),
                                           lambda k: w_out_h[:, k, :], lambda k: w_out_l[:, k, :], HT)
                        last.then_inc(down_psum_attn, 1)

            ffn(0)
            attention()
            ffn(1)

        @block.scalar
        def _(act):
            for c in range(CHUNKS):
                act.dma_start(x_res[:, c * TPC:(c + 1) * TPC], x_tiles[:, c * TPC:(c + 1) * TPC]).then_inc(x_loaded[c], 16)
            nc.scalar.preload_act_table(ACT.Silu)

            def x_high(g, region):
                act.wait_ge(xt_psum, g + 1)
                for k in range(KD):
                    last = nc.scalar.copy(xt_h[:, region, k * CHUNK:(k + 1) * CHUNK], bank_t[k][:, :])
                last.then_inc(xh_ready, 1)

            def split_high(s, par):
                nc.scalar.copy(w_gu_h[:, par], w_raw_gu[:, bass.ds(s, 1)].rearrange("p o k n -> p (o k) n") if not isinstance(s, int) else w_raw_gu[:, s])
                nc.scalar.copy(w_d_h[:, par], w_raw_d[:, bass.ds(s, 1)].rearrange("p o k n -> p (o k) n") if not isinstance(s, int) else w_raw_d[:, s]).then_inc(wh_ready, 1)

            def unit(layer, u, c, f):
                act.wait_ge(gu_psum, n_uf(layer, u, f))
                nc.scalar.activation(work[:, f, :], bank_g[f][:, :], ACT.Silu).then_inc(silu_ready, 1)
                act.wait_ge(mid_ready, n_uf(layer, u, f))
                nc.scalar.copy(mid_h[:, c % 2, f, :], work[:, 2 + f, :]).then_inc(mh_ready, 1)

            def router_tanh_z(layer, c):
                act.wait_ge(logits_read, layer * CHUNKS + c + 1)
                nc.scalar.activation(rt[:, 1], rt[:, 0], ACT.Tanh, scale=half_inv_temp[:, 0:1]).then_inc(tanh_z, 1)

            def router_tanh_d(layer, c):
                act.wait_ge(dist_ready, layer * CHUNKS + c + 1)
                nc.scalar.activation(rt[:, 4], rt[:, 3], ACT.Tanh, scale=1.0 / (2 * 0.1))
                nc.scalar.activation(rt[:, 5], rt[:, 3], ACT.Tanh, scale=1.0 / (2 * 0.3)).then_inc(tanh_d, 1)

            def ffn(layer):
                if layer == 0:
                    act.wait_ge(slot_loaded[0], N_SLOT_LOADS)
                    split_high(0, 0)
                    x_high(0, 0)
                for u in range(2 * CHUNKS):
                    c = u % CHUNKS
                    unit(layer, u, c, 0)
                    if u < CHUNKS:
                        router_tanh_z(layer, c)
                    unit(layer, u, c, 1)
                    if u + 1 < CHUNKS:
                        x_high(g_of(layer, u + 1), u + 1)
                    if u < CHUNKS:
                        router_tanh_d(layer, c)
                    if u in (1, CHUNKS + 1):
                        s = u // CHUNKS + 1
                        if layer == 0:
                            act.wait_ge(slot_loaded[s], N_SLOT_LOADS if s == 1 else N_SLOT_LOADS * (E - 2))
                        act.wait_ge(down_psum, max(n_down(layer, (s - 1) * CHUNKS - 1, 1), 1))
                        split_high(s, s % 2)
                    if u == 2 * CHUNKS - 1 and layer == 0:
                        act.wait_ge(attn_loaded, N_ATTN_LOADS)
                        nc.scalar.copy(w_hid_h[:, :, :], w_hid_raw)
                        nc.scalar.copy(w_out_h[:, :, :], w_out_raw)
                        nc.scalar.copy(w_qk_h[:, :, :], w_qk_raw[:, :, :]).then_inc(attn_wh_ready, 1)
                if layer == 0:
                    act.wait_ge(lora_added, 3 * NL)
                with act.Fori(1, E // 2) as pair:
                    for j in range(2 * CHUNKS):
                        c = j % CHUNKS
                        u = pair * (2 * CHUNKS) + j
                        unit(layer, u, c, 0)
                        unit(layer, u, c, 1)
                        if c == 1:
                            s = pair * 2 + (j // CHUNKS + 1)
                            act.wait_ge(down_psum, n_down(layer, pair * (2 * CHUNKS) + (j - 2), 1))
                            split_high(s % E, (j // CHUNKS + 1) % 2)

            def attention():
                x_high(CHUNKS, 0)
                with act.Fori(0, CHUNKS) as c:
                    act.wait_ge(qk_psum, c + 1)
                    nc.scalar.activation(work[:, 0, :], bank_g[0][:, :], ACT.Silu, bias=vecs[:, 0:1]).then_inc(qk_ready, 1)
                    for i in range(2):
                        act.wait_ge(q_k_ready, c * 2 + (i + 1))
                        nc.scalar.copy(mid_h[:, 0, i, :], work[:, 1 + i, :]).then_inc(qkh_ready, 1)
                    for t in range(TPC):
                        w = work[:, 3 + t % 3, :]
                        act.wait_ge(vb_ready, c * TPC + (t + 1))
                        nc.scalar.activation(w, w, ACT.Silu).then_inc(v_ready, 1)
                        r, o = v_region(t)
                        act.wait_ge(v_ready, c * TPC + (t + 1))
                        nc.scalar.copy(xt_h[:, r, o:o + HID], w).then_inc(vh_ready, 1)
                    g_bank = [bank_u[0], bank_g[1], bank_u[1], bank_g[0]]

                    def gate(h):
                        act.wait_ge(gate_psum, c * HT + (h + 1))
                        nc.scalar.activation(gate_t[:, h, :], g_bank[h][:, :], ACT.Silu, bias=bias_g[:, h:h + 1]).then_inc(gate_ready, 1)

                    gate(0)
                    gate(1)
                    for b in range(BPC):
                        act.wait_ge(sim_psum, c * 2 + (b + 1))
                        nc.scalar.activation(work[:, b, :], bank_t[b][:, :], ACT.Relu, scale=1.0 / SEQ).then_inc(relu_ready, 1)
                    for b in range(BPC):
                        act.wait_ge(sq_ready, c * 2 + (b + 1))
                        nc.scalar.copy(mid_h[:, 1, b, :], work[:, b, :]).then_inc(ah_ready, 1)
                    gate(2)
                    gate(3)
                    x_high(c + (CHUNKS + 1), 0)
                    for n in range(4):
                        r, o = gated_region(2 * (n % 2), n // 2)
                        act.wait_ge(og_ready, c * 4 + (n + 1))
                        nc.scalar.copy(xt_h[:, r, o:o + CHUNK], work[:, 2 + n, :]).then_inc(oh_ready, 1)

            ffn(0)
            attention()
            ffn(1)

        @block.gpsimd
        def _(pool):
            nc.gpsimd.memset(ident[:, :], 0.0).then_inc(pool_step, 1)
            for s in range(E):
                last = nc.gpsimd.memset(tie_key[:, :, s:s + 1], float(E - SLOT_EXPERT[s]))
            last.then_inc(ident_ready, 1)
            pool.wait_ge(pool_step, 1)
            nc.gpsimd.affine_select(out=ident[:, :], in_=ident[:, :], compare_op=ALU.not_equal, fill=1.0, base=0,
                                    pattern=[[-1, P]], channel_multiplier=1).then_inc(ident_ready, 1)

            def low(dst, src, high):
                return nc.gpsimd.tensor_tensor(dst, src, high.bitcast(F32), ALU.subtract)

            def split_low(s, par, n):
                pool.wait_ge(wh_ready, n)
                gu = w_raw_gu[:, s] if isinstance(s, int) else w_raw_gu[:, bass.ds(s, 1)].rearrange("p o k n -> p (o k) n")
                dn = w_raw_d[:, s] if isinstance(s, int) else w_raw_d[:, bass.ds(s, 1)].rearrange("p o k n -> p (o k) n")
                low(w_gu_l[:, par], gu, w_gu_h[:, par])
                low(w_d_l[:, par], dn, w_d_h[:, par]).then_inc(wl_ready, 1)

            def unit(layer, u, c, f):
                pool.wait_ge(mh_ready, n_uf(layer, u, f))
                low(mid_l[:, c % 2, f, :], work[:, 2 + f, :], mid_h[:, c % 2, f, :]).then_inc(ml_ready, 1)

            def ffn(layer):
                if layer == 0:
                    split_low(0, 0, 1)
                for u in range(2 * CHUNKS):
                    c = u % CHUNKS
                    unit(layer, u, c, 0)
                    unit(layer, u, c, 1)
                    if u in (1, CHUNKS + 1):
                        s = u // CHUNKS + 1
                        split_low(s, s % 2, layer * E + s + 1)
                    if u == 2 * CHUNKS - 1 and layer == 0:
                        pool.wait_ge(attn_wh_ready, 1)
                        low(w_hid_l[:, :, :], w_hid_raw, w_hid_h[:, :, :])
                        low(w_out_l[:, :, :], w_out_raw, w_out_h[:, :, :])
                        low(w_qk_l[:, :, :], w_qk_raw[:, :, :], w_qk_h[:, :, :]).then_inc(attn_wl_ready, 1)
                with pool.Fori(1, E // 2) as pair:
                    for j in range(2 * CHUNKS):
                        c = j % CHUNKS
                        u = pair * (2 * CHUNKS) + j
                        unit(layer, u, c, 0)
                        unit(layer, u, c, 1)
                        if c == 1:
                            s = pair * 2 + (j // CHUNKS + 1)
                            split_low(s % E, (j // CHUNKS + 1) % 2, s + (layer * E + 1))

            def attention():
                with pool.Fori(0, CHUNKS) as c:
                    for i in range(2):
                        pool.wait_ge(qkh_ready, c * 2 + (i + 1))
                        low(mid_l[:, 0, i, :], work[:, 1 + i, :], mid_h[:, 0, i, :]).then_inc(qkl_ready, 1)
                    for t in range(TPC):
                        r, o = v_region(t)
                        pool.wait_ge(vh_ready, c * TPC + (t + 1))
                        low(xt_l[:, r, o:o + HID], work[:, 3 + t % 3, :], xt_h[:, r, o:o + HID]).then_inc(vl_ready, 1)
                        if t == 1:
                            nc.gpsimd.tensor_tensor(xn[:, :, :], xn[:, :, :], bias_o[:, :].unsqueeze(1).to_broadcast([P, TPC, D]), ALU.add).then_inc(pool_step, 1)
                            pool.wait_ge(pool_step, c + 2)
                        if t == 2:
                            rows = x_res[:, bass.ds(c * TPC, TPC), :]
                            nc.gpsimd.tensor_tensor(rows, rows, xn[:, :, :], ALU.add).then_inc(resid_ready, 1)
                    for b in range(BPC):
                        pool.wait_ge(ah_ready, c * 2 + (b + 1))
                        low(mid_l[:, 1, b, :], work[:, b, :], mid_h[:, 1, b, :]).then_inc(al_ready, 1)
                    for n in range(4):
                        r, o = gated_region(2 * (n % 2), n // 2)
                        pool.wait_ge(oh_ready, c * 4 + (n + 1))
                        low(xt_l[:, r, o:o + CHUNK], work[:, 2 + n, :], xt_h[:, r, o:o + CHUNK]).then_inc(ol_ready, 1)

            ffn(0)
            attention()
            ffn(1)

        @block.vector
        def _(dve):
            step = [0, 0]

            def ordered(ins):
                step[1] += 1
                ins.then_inc(dve_step, 1)
                dve.wait_ge(dve_step, step[0] + step[1])

            def layernorm(g, chunk, tile):
                for t in range(TPC):
                    last = nc.vector.bn_stats(bn6[:, t, :], tile(t))
                ordered(last)
                v, y, a, b = nw[:, 0], nw[:, 1], nw[:, 2], nw[:, 3]
                nc.vector.tensor_tensor(mv[:, :, 0:2], bn6[:, :, 1:3], bn6[:, :, 4:6], ALU.add)
                ordered(nc.vector.tensor_tensor(a, bn6[:, :, 1], bn6[:, :, 4], ALU.subtract))
                nc.vector.scalar_tensor_tensor(out=b, in0=a, scalar=0.25, in1=a, op0=ALU.mult, op1=ALU.mult)
                nc.vector.tensor_scalar(v, mv[:, :, 1], 1.0 / D, EPS, ALU.mult, ALU.add)
                ordered(nc.vector.tensor_scalar(mv[:, :, 0], mv[:, :, 0], 0.5, None, ALU.mult))
                ordered(nc.vector.tensor_tensor(v, v, b, ALU.add))
                ordered(nc.vector.tensor_scalar(a.bitcast(I32), v.bitcast(I32), 1, None, ALU.logical_shift_right))
                ordered(nc.vector.tensor_scalar(y.bitcast(I32), a.bitcast(I32), -1.0, float(0x5f3759df), ALU.mult, ALU.add))
                for _ in range(3):
                    ordered(nc.vector.tensor_tensor(a, y, y, ALU.mult))
                    ordered(nc.vector.scalar_tensor_tensor(out=b, in0=a, scalar=-0.5, in1=v, op0=ALU.mult, op1=ALU.mult))
                    ordered(nc.vector.scalar_tensor_tensor(out=y, in0=b, scalar=1.5, in1=y, op0=ALU.add, op1=ALU.mult))
                if not (isinstance(g, int) and g == 0):
                    dve.wait_ge(xt_psum, g)
                for t in range(TPC):
                    last = nc.vector.tensor_scalar(xn[:, t, :], tile(t), mv[:, t, 0:1], y[:, t:t + 1], ALU.subtract, ALU.mult)
                last.then_inc(xn_ready, 1)

            def x_low(g, region):
                dve.wait_ge(xh_ready, g + 1)
                for k in range(KD):
                    o = slice(k * CHUNK, (k + 1) * CHUNK)
                    last = nc.vector.tensor_tensor(xt_l[:, region, o], bank_t[k][:, :], xt_h[:, region, o].bitcast(F32), ALU.subtract)
                last.then_inc(xl_ready, 1)

            def mid(layer, u, f):
                dve.wait_ge(silu_ready, n_uf(layer, u, f))
                if not (layer == 0 and isinstance(u, int) and u == 0):
                    dve.wait_ge(ml_ready, n_uf(layer, u, f) - KF)
                nc.vector.tensor_tensor(work[:, 2 + f, :], work[:, f, :], bank_u[f][:, :], ALU.mult).then_inc(mid_ready, 1)

            def add_down(layer, u, c, weight):
                for b in range(2):
                    dve.wait_ge(down_psum, n_down(layer, u, b))
                    if not isinstance(u, int) or u >= CHUNKS:
                        dve.wait_ge(added, n_added(layer, u, b) - 2 * CHUNKS)
                    for t in (2 * b, 2 * b + 1):
                        rows = x_res[:, c * TPC + t, :]
                        last = nc.vector.scalar_tensor_tensor(out=rows, in0=bank_d[b][:, (t % 2) * D:(t % 2 + 1) * D],
                                                              scalar=weight(c * TPC + t), in1=rows, op0=ALU.mult, op1=ALU.add)
                    last.then_inc(added, 1)

            def read_logits(layer, c):
                dve.wait_ge(logits_psum, layer * CHUNKS + c + 1)
                halves = bank_t[0][:, 0:TPC * 2 * E].rearrange("p (t a e) -> p t e a", t=TPC, a=2)
                nc.vector.tensor_reduce(rt[:, 0], halves, axis=AX.X, op=ALU.add).then_inc(logits_read, 1)

            def router_distance(layer, c):
                dve.wait_ge(tanh_z, layer * CHUNKS + c + 1)
                inh, d = rt[:, 2], rt[:, 3]
                ordered(nc.vector.tensor_scalar(inh, rt[:, 1], 0.5, 0.5, ALU.mult, ALU.add))
                diff = rt[:, 11]
                ordered(nc.vector.tensor_scalar(diff, inh, GOLDEN_CENTER, None, ALU.subtract))
                nc.vector.scalar_tensor_tensor(out=d, in0=diff, scalar=-1.0, in1=diff, op0=ALU.mult, op1=ALU.max).then_inc(dist_ready, 1)

            def router_weights(layer, c):
                inh, both = rt[:, 2], rt[:, 4:6]
                w, fb = rt[:, 4], rt[:, 5]
                zone, key, sel1, sel2, fb2 = rt[:, 6], rt[:, 7], rt[:, 8], rt[:, 9], rt[:, 10]

                def per_token(i):
                    return rs[:, i].unsqueeze(2).to_broadcast([P, TPC, E])

                nc.vector.tensor_scalar(zone, inh, GOLDEN_UPPER, None, ALU.is_le)
                dve.wait_ge(tanh_d, layer * CHUNKS + c + 1)
                ordered(nc.vector.tensor_scalar(both, both, 1.0, None, ALU.add))
                ordered(nc.vector.reciprocal(both, both))
                ordered(nc.vector.tensor_scalar(both, both, 2.0, -1.0, ALU.mult, ALU.add))
                ordered(nc.vector.scalar_tensor_tensor(out=zone, in0=inh, scalar=GOLDEN_LOWER, in1=zone, op0=ALU.is_ge, op1=ALU.mult))
                nc.vector.tensor_reduce(rs[:, 1], fb, axis=AX.X, op=ALU.max)
                ordered(nc.vector.tensor_tensor(w, w, zone, ALU.mult))
                ordered(nc.vector.tensor_reduce(rs[:, 0], w, axis=AX.X, op=ALU.add))
                for sel, src in ((sel1, fb), (sel2, fb2)):
                    ordered(nc.vector.tensor_tensor(key, src, per_token(1), ALU.is_ge))
                    ordered(nc.vector.tensor_tensor(key, key, tie_key[:, :, :], ALU.mult))
                    ordered(nc.vector.tensor_reduce(rs[:, 2], key, axis=AX.X, op=ALU.max))
                    ordered(nc.vector.tensor_tensor(sel, key, per_token(2), ALU.is_equal))
                    if src is fb:
                        ordered(nc.vector.scalar_tensor_tensor(out=fb2, in0=sel, scalar=-4.0, in1=fb, op0=ALU.mult, op1=ALU.add))
                        ordered(nc.vector.tensor_reduce(rs[:, 1], fb2, axis=AX.X, op=ALU.max))
                nc.vector.tensor_scalar(rs[:, 0], rs[:, 0], 1e-8, None, ALU.is_lt)
                ordered(nc.vector.tensor_tensor(sel1, sel1, sel2, ALU.add))
                ordered(nc.vector.tensor_tensor(fb, fb, sel1, ALU.mult))
                ordered(nc.vector.tensor_reduce(rs[:, 3], fb, axis=AX.X, op=ALU.add))
                ordered(nc.vector.tensor_scalar(rs[:, 3], rs[:, 3], 1e-8, None, ALU.max))
                ordered(nc.vector.reciprocal(rs[:, 3], rs[:, 3]))
                ordered(nc.vector.tensor_tensor(rs[:, 3], rs[:, 3], rs[:, 0], ALU.mult))
                ordered(nc.vector.tensor_tensor(fb, fb, per_token(3), ALU.mult))
                ordered(nc.vector.tensor_tensor(w, w, fb, ALU.add))
                ordered(nc.vector.tensor_reduce(rs[:, 1], w, axis=AX.X, op=ALU.add))
                ordered(nc.vector.tensor_scalar(rs[:, 1], rs[:, 1], 1e-8, None, ALU.max))
                ordered(nc.vector.reciprocal(rs[:, 1], rs[:, 1]))
                ordered(nc.vector.tensor_scalar(rs[:, 1], rs[:, 1], 0.5, None, ALU.mult))
                ordered(nc.vector.tensor_tensor(route[:, c * TPC:(c + 1) * TPC, :], w, per_token(1), ALU.mult))

            def low_rank():
                for n, (i, e) in enumerate([(i, e) for i in range(3) for e in range(NL)]):
                    s = E - NL + e
                    dve.wait_ge(lora_tr_psum, n + 1)
                    nc.vector.tensor_copy(lora_t[:, n % 2], bank_t[0][0:RANK, 0:2 * P].rearrange("p (k n) -> p k n", k=2)).then_inc(lora_tr, 1)
                    dst = w_raw_d[:, s] if i == 2 else w_raw_gu[:, s, :, i * F:(i + 1) * F]
                    dve.wait_ge(lora_psum, n + 1)
                    nc.vector.tensor_tensor(dst, dst, bank_t[1][:, :].rearrange("p (k n) -> p k n", k=2), ALU.add).then_inc(lora_added, 1)

            def ffn(layer):
                def tile(c):
                    return lambda t: x_res[:, c * TPC + t, :]

                if layer == 0:
                    dve.wait_ge(x_loaded[0], 16)
                    layernorm(0, 0, tile(0))
                    dve.wait_ge(router_loaded, 48)
                    nc.vector.tensor_copy(wr_hl[:, :, 0, :], wr_raw[:, :, :])
                    ordered(nc.vector.reciprocal(half_inv_temp[:, :], temp[:, :]))
                    ordered(nc.vector.tensor_scalar(half_inv_temp[:, :], half_inv_temp[:, :], 0.5, None, ALU.mult))
                    nc.vector.tensor_tensor(wr_hl[:, :, 1, :], wr_raw[:, :, :], wr_hl[:, :, 0, :].bitcast(F32), ALU.subtract).then_inc(router_w_ready, 1)
                    dve.wait_ge(ident_ready, 2)
                    x_low(0, 0)
                for u in range(2 * CHUNKS):
                    c = u % CHUNKS
                    if u + 1 < CHUNKS:
                        if layer == 0:
                            dve.wait_ge(x_loaded[u + 1], 16)
                        layernorm(g_of(layer, u + 1), u + 1, tile(u + 1))
                    mid(layer, u, 0)
                    if u < CHUNKS:
                        read_logits(layer, c)
                        router_distance(layer, c)
                    mid(layer, u, 1)
                    if u + 1 < CHUNKS:
                        x_low(g_of(layer, u + 1), u + 1)
                    if u < CHUNKS:
                        router_weights(layer, c)
                    if u > 0:
                        s, cd = (u - 1) // CHUNKS, (u - 1) % CHUNKS
                        add_down(layer, u - 1, cd, lambda n: route[:, n, s:s + 1])
                    if u == CHUNKS and layer == 0:
                        dve.wait_ge(slot_loaded[2], N_SLOT_LOADS * (E - 2))
                        low_rank()
                with dve.Fori(1, E // 2) as pair:
                    for j in range(2 * CHUNKS):
                        u = pair * (2 * CHUNKS) + j
                        mid(layer, u, 0)
                        mid(layer, u, 1)
                        s = pair * 2 + (j - 1) // CHUNKS
                        add_down(layer, u - 1, (j - 1) % CHUNKS, lambda n: route[:, n, bass.ds(s, 1)])
                if layer == 0:
                    layernorm(CHUNKS, 0, tile(0))
                add_down(layer, UNITS - 1, CHUNKS - 1, lambda n: route[:, n, E - 1:E])

            def attention():
                x_low(CHUNKS, 0)
                before = step[1]
                with dve.Fori(0, CHUNKS) as c:
                    step[0], step[1] = c * LN_STEPS, before
                    for i in range(2):
                        if i == 0:
                            dve.wait_ge(qk_ready, c + 1)
                        nc.vector.tensor_scalar(work[:, 1 + i, :], work[:, 0, :], vecs[:, 1 + 2 * i:2 + 2 * i],
                                                vecs[:, 2 + 2 * i:3 + 2 * i], ALU.mult, ALU.add).then_inc(q_k_ready, 1)
                    v_bank = [bank_u[0], bank_g[1], bank_u[1], bank_g[0]]
                    for t in range(TPC):
                        dve.wait_ge(v_psum, c * TPC + (t + 1))
                        if t == 3:
                            dve.wait_ge(vl_ready, c * TPC + 1)
                        nc.vector.tensor_tensor(work[:, 3 + t % 3, :], v_bank[t][:, :], bias_v[:, :], ALU.add).then_inc(vb_ready, 1)
                    nxt = (c + 1) % CHUNKS
                    dve.wait_ge(resid_ready, c + 1)
                    layernorm(c + (CHUNKS + 1), nxt, lambda t: x_res[:, bass.ds(nxt * TPC + t, 1), :].rearrange("p o d -> p (o d)"))
                    assert step[1] - before == LN_STEPS
                    for b in range(BPC):
                        dve.wait_ge(relu_ready, c * 2 + (b + 1))
                        nc.vector.tensor_tensor(work[:, b, :], work[:, b, :], work[:, b, :], ALU.mult).then_inc(sq_ready, 1)
                    x_low(c + (CHUNKS + 1), 0)
                    av_bank = [bank_u[0], bank_g[1], bank_u[1], bank_g[0]]
                    for n in range(4):
                        b, hp = n // 2, n % 2
                        dve.wait_ge(av_psum, c * 4 + (n + 1))
                        nc.vector.tensor_tensor(work[:, 2 + n, :].rearrange("p (h i) -> p h i", h=2),
                                                av_bank[n][:, :].rearrange("p (h i) -> p h i", h=2),
                                                gate_t[:, 2 * hp:2 * hp + 2, b * SEQ:(b + 1) * SEQ], ALU.mult).then_inc(og_ready, 1)
                    for b in range(BPC):
                        dve.wait_ge(down_psum_attn, c * 2 + (b + 1))
                        rows = x_res[:, bass.ds(c * TPC + 2 * b, 2), :]
                        nc.vector.tensor_tensor(rows, bank_d[b][:, :].rearrange("p (t d) -> p t d", t=2), rows, ALU.add).then_inc(added, 1)
                step[0], step[1] = 0, before + CHUNKS * LN_STEPS

            LN_STEPS = 6 + 9
            ffn(0)
            attention()
            ffn(1)


_INS = ['L0_attn_x', 'L0_attn_W_hidden', 'L0_attn_b_hidden', 'L0_attn_W_qk', 'L0_attn_b_qk', 'L0_attn_gamma_q',
        'L0_attn_beta_q', 'L0_attn_gamma_k', 'L0_attn_beta_k', 'L0_attn_W_out', 'L0_attn_b_out', 'L0_ffn_Wg',
        'L0_ffn_Wu', 'L0_ffn_Wd', 'L0_ffn_Ga', 'L0_ffn_Gb', 'L0_ffn_Ua', 'L0_ffn_Ub', 'L0_ffn_Da', 'L0_ffn_Db',
        'L0_ffn_Wr', 'L0_ffn_temperature']


def kernel(**inputs):
    import numpy as _np
    import concourse.bacc as _bacc
    from concourse.bass_utils import run_bass_kernel_spmd as _run

    nc = _bacc.Bacc("TRN2", target_bir_lowering=False, num_devices=1)
    arrays, args = {}, []
    for name in _INS:
        a = _np.ascontiguousarray(inputs[name])
        arrays[f"in_{name}"] = a
        args.append(nc.dram_tensor(f"in_{name}", a.shape, F32, kind="ExternalInput").ap())
    args.append(nc.dram_tensor("out_x", (SEQS, SEQ, D), F32, kind="ExternalOutput").ap())
    build(nc, *args)
    r = _run(nc, [arrays], core_ids=[0])
    return r.results[0]["out_x"]
```

```python
import math
from contextlib import ExitStack

import concourse.bass as bass
from concourse import mybir
from concourse.alu_op_type import AluOpType as ALU

F32 = mybir.dt.float32
F32R = mybir.dt.float32r
I32 = mybir.dt.int32
ACT = mybir.ActivationFunctionType
AX = mybir.AxisListType

P = 128
SEQS, SEQ, D = 8, 256, 256
TOKENS = SEQS * SEQ
CHUNK = 512
CHUNKS = TOKENS // CHUNK
TPC = CHUNK // P
TILES = TOKENS // P
KD = D // P
E, F, NL, RANK = 8, 256, 2, 64
KF = F // P
HID, QK = 512, 128
HT = HID // P
BPC = CHUNK // SEQ
UNITS = E * CHUNKS
EPS = 1e-5
SLOT_EXPERT = [(s + NL) % E for s in range(E)]

GOLDEN_CENTER = 1.0 / math.e
GOLDEN_LOWER = 0.5 - math.log(4.0 / 3.0)
GOLDEN_UPPER = 0.5


def build(nc, x_in, w_hidden, b_hidden, w_qk, b_qk, gamma_q, beta_q, gamma_k, beta_k, w_out, b_out,
          wg, wu, wd, ga, gb, ua, ub, da, db, wr, temperature, out):
    ctx = ExitStack()
    with ctx:
        def sb(name, shape, dt=F32):
            return ctx.enter_context(nc.sbuf_tensor(name, shape, dt))

        def ps(name):
            return ctx.enter_context(nc.psum_tensor(name, [P, 512], F32))

        def sem(name):
            return ctx.enter_context(nc.semaphore(name))

        x_res = sb("x_res", [P, TILES, D])
        xn = sb("xn", [P, TPC, D])
        xt_h = sb("xt_h", [P, CHUNKS + 1, 2 * CHUNK], F32R)
        xt_l = sb("xt_l", [P, CHUNKS + 1, 2 * CHUNK], F32R)
        mid_h = sb("mid_h", [P, 2, KF, CHUNK], F32R)
        mid_l = sb("mid_l", [P, 2, KF, CHUNK], F32R)
        w_raw_gu = sb("w_raw_gu", [P, E, KD, 2 * F])
        w_raw_d = sb("w_raw_d", [P, E, KF, D])
        w_gu_h = sb("w_gu_h", [P, 2, KD, 2 * F], F32R)
        w_gu_l = sb("w_gu_l", [P, 2, KD, 2 * F], F32R)
        w_d_h = sb("w_d_h", [P, 2, KF, D], F32R)
        w_d_l = sb("w_d_l", [P, 2, KF, D], F32R)
        w_hid_h = sb("w_hid_h", [P, KD, 2 * HID], F32R)
        w_hid_l = sb("w_hid_l", [P, KD, 2 * HID], F32R)
        w_out_h = sb("w_out_h", [P, HT, D], F32R)
        w_out_l = sb("w_out_l", [P, HT, D], F32R)
        w_qk_h = sb("w_qk_h", [P, KD, QK], F32R)
        w_qk_l = sb("w_qk_l", [P, KD, QK], F32R)
        w_qk_raw = sb("w_qk_raw", [P, KD, QK])
        gate_t = sb("gate_t", [P, HT, CHUNK])
        w_hid_raw = gate_t[:, :, :].rearrange("p h c -> p (h c)").rearrange("p (k n) -> p k n", k=KD)
        work = sb("work", [P, 6, CHUNK])
        w_out_raw = work[:, 4:6, :].rearrange("p a b -> p (a b)").rearrange("p (h n) -> p h n", h=HT)
        ident = sb("ident", [P, P])
        bias_v = sb("bias_v", [P, HID])
        bias_o = sb("bias_o", [P, D])
        bias_g = sb("bias_g", [P, HT])
        vecs = sb("vecs", [P, 5])
        spare = gate_t[:, :, :].rearrange("p h c -> p (h c)")
        lora_a = work[:, 4:6, :].rearrange("p a b -> p (a b)")[:, 0:3 * NL * 2 * RANK].rearrange(
            "p (i e k r) -> p i e k r", i=3, e=NL, k=2)
        lora_b = spare[0:RANK, 0:3 * NL * F].rearrange("p (i e f) -> p i e f", i=3, e=NL)
        lora_t = sb("lora_t", [RANK, 3, 2 * NL * P])
        wr_raw = sb("wr_raw", [P, KD, E])
        wr_hl = sb("wr_hl", [P, KD, 2, E], F32R)
        temp = sb("temp", [P, 1])
        half_inv_temp = sb("half_inv_temp", [P, 1])
        bn6 = sb("bn6", [P, TPC, 6])
        mv = sb("mv", [P, TPC, 2])
        nw = sb("nw", [P, 6, TPC])
        route = sb("route", [P, TILES, E])
        rt = sb("rt", [P, 12, TPC, E])
        rs = sb("rs", [P, 2, TPC])
        top8 = sb("top8", [P, TPC, 8])

        bank_g = [ps("bank_g0"), ps("bank_g1")]
        bank_u = [ps("bank_u0"), ps("bank_u1")]
        bank_d = [ps("bank_d0"), ps("bank_d1")]
        bank_t = [ps("bank_t0"), ps("bank_t1")]

        x_loaded = [sem(f"x_loaded{c}") for c in range(CHUNKS)]
        slot_loaded = [sem("slot0_loaded"), sem("slot1_loaded"), sem("slots_rest_loaded")]
        router_loaded = sem("router_loaded")
        lora_a_loaded = sem("lora_a_loaded")
        lora_b_loaded = sem("lora_b_loaded")
        attn_loaded = sem("attn_loaded")
        out_stored = sem("out_stored")
        ident_ready = sem("ident_ready")
        pool_step = sem("pool_step")
        dve_step = sem("dve_step")
        router_w_ready = sem("router_w_ready")
        xn_ready = sem("xn_ready")
        xt_psum = sem("xt_psum")
        xh_ready = sem("xh_ready")
        xl_ready = sem("xl_ready")
        logits_psum = sem("logits_psum")
        logits_read = sem("logits_read")
        tanh_z = sem("tanh_z")
        dist_ready = sem("dist_ready")
        tanh_d = sem("tanh_d")
        wh_ready = sem("wh_ready")
        wl_ready = sem("wl_ready")
        gu_psum = sem("gu_psum")
        silu_ready = sem("silu_ready")
        mid_ready = sem("mid_ready")
        mh_ready = sem("mh_ready")
        ml_ready = sem("ml_ready")
        down_psum = sem("down_psum")
        added = sem("added")
        lora_tr_psum = sem("lora_tr_psum")
        lora_tr = sem("lora_tr")
        lora_psum = sem("lora_psum")
        lora_added = sem("lora_added")
        attn_wh_ready = sem("attn_wh_ready")
        attn_wl_ready = sem("attn_wl_ready")
        qk_psum = sem("qk_psum")
        qk_ready = sem("qk_ready")
        q_k_ready = sem("q_k_ready")
        qkh_ready = sem("qkh_ready")
        qkl_ready = sem("qkl_ready")
        v_psum = sem("v_psum")
        vb_ready = sem("vb_ready")
        v_ready = sem("v_ready")
        vh_ready = sem("vh_ready")
        vl_ready = sem("vl_ready")
        gate_psum = sem("gate_psum")
        gate_ready = sem("gate_ready")
        sim_psum = sem("sim_psum")
        relu_ready = sem("relu_ready")
        sq_ready = sem("sq_ready")
        ah_ready = sem("ah_ready")
        al_ready = sem("al_ready")
        av_psum = sem("av_psum")
        og_ready = sem("og_ready")
        oh_ready = sem("oh_ready")
        ol_ready = sem("ol_ready")
        down_psum_attn = sem("down_psum_attn")
        resid_ready = sem("resid_ready")
        bias_added = sem("bias_added")

        L_ADDED = [0, 2 * UNITS + 2 * CHUNKS]
        A_ADDED = 2 * UNITS

        def n_uf(layer, u, f):
            return u * KF + (layer * UNITS * KF + f + 1)

        def n_down(layer, u, b):
            return u * 2 + (layer * UNITS * 2 + b + 1)

        def n_added(layer, u, b):
            return u * 2 + (L_ADDED[layer] + b + 1)

        def g_of(layer, c):
            return 2 * CHUNKS * layer + c

        def w_col(ap, s):
            return ap[:, bass.ds(s, 1)]

        def v_region(t, n=HID):
            return 1 + t // 2, (t % 2) * HID

        def gated_region(h, b):
            return 3 + b, h * SEQ

        block = ctx.enter_context(nc.Block())

        x_tiles = x_in.rearrange("b (h p) d -> p (b h) d", p=P)
        out_tiles = out.rearrange("b (h p) d -> p (b h) d", p=P)

        @block.sync
        def _(sp):
            def load_slot(s, done):
                e = SLOT_EXPERT[s]
                sp.dma_start(w_raw_gu[:, s, :, 0:F], wg[e].rearrange("(k p) f -> p k f", p=P)).then_inc(done, 16)
                sp.dma_start(w_raw_gu[:, s, :, F:2 * F], wu[e].rearrange("(k p) f -> p k f", p=P)).then_inc(done, 16)
                sp.dma_start(w_raw_d[:, s], wd[e].rearrange("(k p) f -> p k f", p=P)).then_inc(done, 16)

            load_slot(0, slot_loaded[0])
            sp.dma_start(wr_raw[:, :, :], wr.rearrange("(k p) e -> p k e", p=P)).then_inc(router_loaded, 16)
            sp.dma_start(temp[:, :], temperature.partition_broadcast(P)).then_inc(router_loaded, 16)
            load_slot(1, slot_loaded[1])
            for i, b in enumerate((gb, ub, db)):
                sp.dma_start(lora_b[:, i], b.rearrange("e r f -> r e f")).then_inc(lora_b_loaded, 16)
            for s in range(2, E):
                load_slot(s, slot_loaded[2])
            sp.wait_ge(lora_added, 3 * NL)
            sp.dma_start(w_hid_raw, w_hidden.rearrange("(k p) n -> p k n", p=P)).then_inc(attn_loaded, 16)
            sp.dma_start(w_out_raw, w_out.rearrange("(h p) n -> p h n", p=P)).then_inc(attn_loaded, 16)
            sp.dma_start(w_qk_raw[:, :, :], w_qk.rearrange("(k p) n -> p k n", p=P)).then_inc(attn_loaded, 16)
            for i, v in enumerate((b_qk, gamma_q, beta_q, gamma_k, beta_k)):
                sp.dma_start(vecs[:, i:i + 1], v.rearrange("(p o) -> p o", o=1)).then_inc(attn_loaded, 16)
            for h in range(HT):
                sp.dma_start(bias_g[:, h:h + 1], b_hidden[HID + h * P:HID + (h + 1) * P].rearrange("(p o) -> p o", o=1)).then_inc(attn_loaded, 16)
            sp.dma_start(bias_v[:, :], b_hidden[0:HID].partition_broadcast(P)).then_inc(attn_loaded, 16)
            sp.dma_start(bias_o[:, :], b_out.partition_broadcast(P)).then_inc(attn_loaded, 16)
            for c in range(CHUNKS):
                sp.wait_ge(added, n_added(1, UNITS - CHUNKS + c, 1))
                sp.dma_start(out_tiles[:, c * TPC:(c + 1) * TPC], x_res[:, c * TPC:(c + 1) * TPC]).then_inc(out_stored, 16)
            sp.wait_ge(out_stored, 16 * CHUNKS)

        N_ATTN_LOADS = 16 * (3 + 5 + HT + 2)
        N_LORA_A_LOADS = 16 * 3 * NL
        N_LORA_B_LOADS = 16 * 3
        N_SLOT_LOADS = 16 * 3

        lora_bank = [bank_d[0], bank_d[1], bank_u[1]]

        @block.tensor
        def _(pe):
            def transposes(g):
                pe.wait_ge(xn_ready, g + 1)
                for k in range(KD):
                    for t in range(TPC):
                        last = nc.tensor.transpose(bank_t[k][:, t * P:(t + 1) * P], xn[:, t, k * P:(k + 1) * P], ident[:, :])
                last.then_inc(xt_psum, 1)

            def logits(layer, c):
                g = g_of(layer, c)
                pe.wait_ge(xh_ready, g + 1)
                pe.wait_ge(xl_ready, g + 1)
                if layer == 0 and c == 0:
                    pe.wait_ge(router_w_ready, 1)
                for t in range(TPC):
                    for i, (xt, k) in enumerate([(xt, k) for k in range(KD) for xt in (xt_h, xt_l)]):
                        last = nc.tensor.matmul(bank_t[0][:, t * 2 * E:(t + 1) * 2 * E],
                                                xt[:, c, k * CHUNK + t * P:k * CHUNK + (t + 1) * P],
                                                wr_hl[:, k].rearrange("p a e -> p (a e)"),
                                                start=(i == 0), stop=(i == 2 * KD - 1))
                last.then_inc(logits_psum, 1)

            def gate_up(layer, u, par, c, f):
                if c == 0 and f == 0:
                    s = 0 if isinstance(u, int) and u == 0 else None
                    pe.wait_ge(wh_ready, (u // CHUNKS if isinstance(u, int) else slot_of[0]) + (layer * E + 1))
                    pe.wait_ge(wl_ready, (u // CHUNKS if isinstance(u, int) else slot_of[0]) + (layer * E + 1))
                if isinstance(u, int) and u < CHUNKS and f == 0:
                    pe.wait_ge(xh_ready, g_of(layer, c) + 1)
                    pe.wait_ge(xl_ready, g_of(layer, c) + 1)
                if not (layer == 0 and isinstance(u, int) and u == 0):
                    pe.wait_ge(mid_ready, n_uf(layer, u, f) - KF)
                for bank, col in ((bank_g[f], f * P), (bank_u[f], F + f * P)):
                    for k in range(KD):
                        xh = xt_h[:, c, k * CHUNK:(k + 1) * CHUNK]
                        xl = xt_l[:, c, k * CHUNK:(k + 1) * CHUNK]
                        wh = w_gu_h[:, par, k, col:col + P]
                        wl = w_gu_l[:, par, k, col:col + P]
                        nc.tensor.matmul(bank[:, :], wh, xh, start=(k == 0), stop=False)
                        nc.tensor.matmul(bank[:, :], wh, xl, start=False, stop=False)
                        last = nc.tensor.matmul(bank[:, :], wl, xh, start=False, stop=(k == KD - 1))
                last.then_inc(gu_psum, 1)

            def down(layer, u, par, c, first=False):
                pe.wait_ge(mh_ready, n_uf(layer, u, KF - 1))
                pe.wait_ge(ml_ready, n_uf(layer, u, KF - 1))
                m = c % 2
                for b in range(2):
                    if not first:
                        pe.wait_ge(added, n_added(layer, u, b) - 2)
                    for t in (2 * b, 2 * b + 1):
                        o = bank_d[b][:, (t % 2) * D:(t % 2 + 1) * D]
                        for k in range(KF):
                            mh = mid_h[:, m, k, t * P:(t + 1) * P]
                            ml = mid_l[:, m, k, t * P:(t + 1) * P]
                            nc.tensor.matmul(o, mh, w_d_h[:, par, k, :], start=(k == 0), stop=False)
                            nc.tensor.matmul(o, mh, w_d_l[:, par, k, :], start=False, stop=False)
                            last = nc.tensor.matmul(o, ml, w_d_h[:, par, k, :], start=False, stop=(k == KF - 1))
                    last.then_inc(down_psum, 1)

            def low_rank_transposes():
                pe.wait_ge(ident_ready, 1)
                pe.wait_ge(lora_a_loaded, N_LORA_A_LOADS)
                for i in range(3):
                    for e in range(NL):
                        for k in range(2):
                            n = 2 * e + k
                            last = nc.tensor.transpose(lora_bank[i][0:RANK, n * P:(n + 1) * P], lora_a[:, i, e, k, :], ident[:, :])
                    last.then_inc(lora_tr_psum, 1)

            def low_rank(n):
                i, e = n // NL, n % NL
                if n == 0:
                    pe.wait_ge(lora_tr, 3)
                    pe.wait_ge(lora_b_loaded, N_LORA_B_LOADS)
                    pe.wait_ge(xl_ready, CHUNKS)
                    pe.wait_ge(logits_read, CHUNKS)
                elif n > 1:
                    pe.wait_ge(lora_added, n - 1)
                for k in range(2):
                    m = 2 * e + k
                    last = nc.tensor.matmul(bank_t[n % 2][:, k * F:(k + 1) * F], lora_t[:, i, m * P:(m + 1) * P], lora_b[:, i, e, :],
                                            start=True, stop=True)
                last.then_inc(lora_psum, 1)

            slot_of = [None]

            def ffn(layer):
                if layer == 0:
                    low_rank_transposes()
                    transposes(0)
                for u in range(2 * CHUNKS):
                    c, par = u % CHUNKS, u // CHUNKS
                    gate_up(layer, u, par, c, 0)
                    if u < CHUNKS:
                        logits(layer, c)
                    gate_up(layer, u, par, c, 1)
                    if u + 1 < CHUNKS:
                        pe.wait_ge(logits_read, layer * CHUNKS + c + 1)
                        transposes(g_of(layer, u + 1))
                    if u > 0:
                        down(layer, u - 1, (u - 1) // CHUNKS, (u - 1) % CHUNKS, first=(layer == 0 and u == 1))
                    if layer == 0 and u in (CHUNKS, CHUNKS + 1, CHUNKS + 2):
                        low_rank(2 * (u - CHUNKS))
                        low_rank(2 * (u - CHUNKS) + 1)
                with pe.Fori(1, E // 2 - 1) as pair:
                    for j in range(2 * CHUNKS):
                        c, par = j % CHUNKS, j // CHUNKS
                        slot_of[0] = pair * 2 + par
                        u = pair * (2 * CHUNKS) + j
                        gate_up(layer, u, par, c, 0)
                        gate_up(layer, u, par, c, 1)
                        jd = (j - 1) % (2 * CHUNKS)
                        down(layer, pair * (2 * CHUNKS) + (j - 1), jd // CHUNKS, jd % CHUNKS)
                for u in range(UNITS - 2 * CHUNKS, UNITS):
                    c, par = u % CHUNKS, (u // CHUNKS) % 2
                    gate_up(layer, u, par, c, 0)
                    gate_up(layer, u, par, c, 1)
                    if layer == 0 and u == UNITS - 1:
                        transposes(CHUNKS)
                    down(layer, u - 1, ((u - 1) // CHUNKS) % 2, (u - 1) % CHUNKS)
                down(layer, UNITS - 1, 1, CHUNKS - 1)

            def project(bank, lh, ll, rh, rl, ks):
                for k in range(ks):
                    nc.tensor.matmul(bank, lh(k), rh(k), start=(k == 0), stop=False)
                    nc.tensor.matmul(bank, lh(k), rl(k), start=False, stop=False)
                    last = nc.tensor.matmul(bank, ll(k), rh(k), start=False, stop=(k == ks - 1))
                return last

            def attention():
                pe.wait_ge(attn_wh_ready, 1)
                pe.wait_ge(attn_wl_ready, 1)
                with pe.Fori(0, CHUNKS) as c:
                    def xh(k):
                        return xt_h[:, 0, k * CHUNK:(k + 1) * CHUNK]

                    def xl(k):
                        return xt_l[:, 0, k * CHUNK:(k + 1) * CHUNK]

                    pe.wait_ge(xh_ready, c + (CHUNKS + 1))
                    pe.wait_ge(xl_ready, c + (CHUNKS + 1))
                    project(bank_g[0][:, :], lambda k: w_qk_h[:, k, :], lambda k: w_qk_l[:, k, :], xh, xl, KD).then_inc(qk_psum, 1)
                    v_bank = [bank_u[0], bank_g[1], bank_u[1], bank_g[0]]
                    for t in range(TPC):
                        if t == 3:
                            pe.wait_ge(qk_ready, c + 1)
                        project(v_bank[t][:, :],
                                lambda k: xt_h[:, 0, k * CHUNK + t * P:k * CHUNK + (t + 1) * P],
                                lambda k: xt_l[:, 0, k * CHUNK + t * P:k * CHUNK + (t + 1) * P],
                                lambda k: w_hid_h[:, k, 0:HID], lambda k: w_hid_l[:, k, 0:HID], KD).then_inc(v_psum, 1)

                    def gate(h):
                        pe.wait_ge(vb_ready, c * TPC + (h + 1))
                        col = HID + h * P
                        project(v_bank[h][:, :], lambda k: w_hid_h[:, k, col:col + P],
                                lambda k: w_hid_l[:, k, col:col + P], xh, xl, KD).then_inc(gate_psum, 1)

                    def similarity(b):
                        for j in range(2):
                            o = bank_t[b][:, j * SEQ:(j + 1) * SEQ]
                            ks = slice(b * SEQ + j * P, b * SEQ + (j + 1) * P)
                            qs = slice(b * SEQ, (b + 1) * SEQ)
                            last = project(o, lambda k: mid_h[:, 0, 1, ks], lambda k: mid_l[:, 0, 1, ks],
                                           lambda k: mid_h[:, 0, 0, qs], lambda k: mid_l[:, 0, 0, qs], 1)
                        last.then_inc(sim_psum, 1)

                    gate(0)
                    gate(1)
                    pe.wait_ge(qkh_ready, c * 2 + 2)
                    pe.wait_ge(qkl_ready, c * 2 + 2)
                    similarity(0)
                    similarity(1)
                    gate(2)
                    gate(3)
                    pe.wait_ge(relu_ready, c * 2 + 2)
                    transposes(c + (CHUNKS + 1))
                    av_bank = [bank_u[0], bank_g[1], bank_u[1], bank_g[0]]
                    pe.wait_ge(vh_ready, c * TPC + TPC)
                    pe.wait_ge(vl_ready, c * TPC + TPC)
                    for b in range(BPC):
                        pe.wait_ge(ah_ready, c * 2 + (b + 1))
                        pe.wait_ge(al_ready, c * 2 + (b + 1))
                        for hp in range(2):
                            pe.wait_ge(gate_ready, c * HT + (2 * b + hp + 1))
                            for h in (2 * hp, 2 * hp + 1):
                                def v_part(buf, k):
                                    r, o = v_region(2 * b + k)
                                    return buf[:, r, o + h * P:o + (h + 1) * P]

                                last = project(av_bank[2 * b + hp][:, (h % 2) * SEQ:(h % 2 + 1) * SEQ],
                                               lambda k: v_part(xt_h, k), lambda k: v_part(xt_l, k),
                                               lambda k: mid_h[:, 1, b, k * SEQ:(k + 1) * SEQ],
                                               lambda k: mid_l[:, 1, b, k * SEQ:(k + 1) * SEQ], 2)
                            last.then_inc(av_psum, 1)
                    for b in range(BPC):
                        pe.wait_ge(oh_ready, c * 4 + (2 * b + 2))
                        pe.wait_ge(ol_ready, c * 4 + (2 * b + 2))
                        pe.wait_ge(added, c * 2 + (A_ADDED + b - 1))
                        for t in range(2):
                            def o_part(buf, k):
                                r, o = gated_region(k, b)
                                return buf[:, r, o + t * P:o + (t + 1) * P]

                            last = project(bank_d[b][:, t * D:(t + 1) * D],
                                           lambda k: o_part(xt_h, k), lambda k: o_part(xt_l, k),
                                           lambda k: w_out_h[:, k, :], lambda k: w_out_l[:, k, :], HT)
                        last.then_inc(down_psum_attn, 1)

            ffn(0)
            attention()
            ffn(1)

        @block.scalar
        def _(act):
            for c in range(CHUNKS):
                act.dma_start(x_res[:, c * TPC:(c + 1) * TPC], x_tiles[:, c * TPC:(c + 1) * TPC]).then_inc(x_loaded[c], 16)
                if c == 0:
                    for i, a in enumerate((ga, ua, da)):
                        for e in range(NL):
                            act.dma_start(lora_a[:, i, e], a[e].rearrange("(k p) r -> p k r", p=P)).then_inc(lora_a_loaded, 16)
            nc.scalar.preload_act_table(ACT.Silu)

            def x_high(g, region):
                act.wait_ge(xt_psum, g + 1)
                for k in range(KD):
                    last = nc.scalar.copy(xt_h[:, region, k * CHUNK:(k + 1) * CHUNK], bank_t[k][:, :])
                last.then_inc(xh_ready, 1)

            def split_high(s, par):
                nc.scalar.copy(w_gu_h[:, par], w_raw_gu[:, bass.ds(s, 1)].rearrange("p o k n -> p (o k) n") if not isinstance(s, int) else w_raw_gu[:, s])
                nc.scalar.copy(w_d_h[:, par], w_raw_d[:, bass.ds(s, 1)].rearrange("p o k n -> p (o k) n") if not isinstance(s, int) else w_raw_d[:, s]).then_inc(wh_ready, 1)

            def unit(layer, u, c, f):
                act.wait_ge(gu_psum, n_uf(layer, u, f))
                nc.scalar.activation(work[:, f, :], bank_g[f][:, :], ACT.Silu).then_inc(silu_ready, 1)
                act.wait_ge(mid_ready, n_uf(layer, u, f))
                nc.scalar.copy(mid_h[:, c % 2, f, :], work[:, 2 + f, :]).then_inc(mh_ready, 1)

            def router_tanh_z(layer, c):
                act.wait_ge(logits_read, layer * CHUNKS + c + 1)
                nc.scalar.activation(rt[:, 1], rt[:, 0], ACT.Tanh, scale=half_inv_temp[:, 0:1]).then_inc(tanh_z, 1)

            def router_tanh_d(layer, c):
                act.wait_ge(dist_ready, layer * CHUNKS + c + 1)
                nc.scalar.activation(rt[:, 4], rt[:, 3], ACT.Tanh, scale=1.0 / (2 * 0.1))
                nc.scalar.activation(rt[:, 5], rt[:, 3], ACT.Tanh, scale=1.0 / (2 * 0.3)).then_inc(tanh_d, 1)

            def ffn(layer):
                if layer == 0:
                    for i in range(3):
                        act.wait_ge(lora_tr_psum, i + 1)
                        nc.scalar.copy(lora_t[:, i, :], lora_bank[i][0:RANK, :]).then_inc(lora_tr, 1)
                    act.wait_ge(slot_loaded[0], N_SLOT_LOADS)
                    split_high(0, 0)
                    x_high(0, 0)
                for u in range(2 * CHUNKS):
                    c = u % CHUNKS
                    unit(layer, u, c, 0)
                    if u < CHUNKS:
                        router_tanh_z(layer, c)
                    unit(layer, u, c, 1)
                    if u + 1 < CHUNKS:
                        x_high(g_of(layer, u + 1), u + 1)
                    if u < CHUNKS:
                        router_tanh_d(layer, c)
                    if u in (1, CHUNKS + 1):
                        s = u // CHUNKS + 1
                        if layer == 0:
                            act.wait_ge(slot_loaded[s], N_SLOT_LOADS if s == 1 else N_SLOT_LOADS * (E - 2))
                        act.wait_ge(down_psum, max(n_down(layer, (s - 1) * CHUNKS - 1, 1), 1))
                        split_high(s, s % 2)
                if layer == 0:
                    act.wait_ge(lora_added, 3 * NL)
                with act.Fori(1, E // 2 - 1) as pair:
                    for j in range(2 * CHUNKS):
                        c = j % CHUNKS
                        u = pair * (2 * CHUNKS) + j
                        unit(layer, u, c, 0)
                        unit(layer, u, c, 1)
                        if c == 1:
                            s = pair * 2 + (j // CHUNKS + 1)
                            act.wait_ge(down_psum, n_down(layer, pair * (2 * CHUNKS) + (j - 2), 1))
                            split_high(s, (j // CHUNKS + 1) % 2)
                for u in range(UNITS - 2 * CHUNKS, UNITS):
                    c, s = u % CHUNKS, u // CHUNKS + 1
                    unit(layer, u, c, 0)
                    unit(layer, u, c, 1)
                    if c == 1 and (s < E or layer == 0):
                        act.wait_ge(down_psum, n_down(layer, u - 2, 1))
                        split_high(s % E, s % 2)
                    if layer == 0 and u == UNITS - 2 * CHUNKS:
                        act.wait_ge(attn_loaded, N_ATTN_LOADS)
                        nc.scalar.copy(w_hid_h[:, :, :], w_hid_raw)
                        nc.scalar.copy(w_out_h[:, :, :], w_out_raw)
                        nc.scalar.copy(w_qk_h[:, :, :], w_qk_raw[:, :, :]).then_inc(attn_wh_ready, 1)
                    if layer == 0 and u == UNITS - 1:
                        x_high(CHUNKS, 0)

            def attention():
                with act.Fori(0, CHUNKS) as c:
                    act.wait_ge(qk_psum, c + 1)
                    nc.scalar.activation(work[:, 0, :], bank_g[0][:, :], ACT.Silu, bias=vecs[:, 0:1]).then_inc(qk_ready, 1)
                    for i in range(2):
                        act.wait_ge(q_k_ready, c * 2 + (i + 1))
                        nc.scalar.copy(mid_h[:, 0, i, :], work[:, 1 + i, :]).then_inc(qkh_ready, 1)
                    for t in range(TPC):
                        w = work[:, 3 + t % 3, :]
                        act.wait_ge(vb_ready, c * TPC + (t + 1))
                        nc.scalar.activation(w, w, ACT.Silu).then_inc(v_ready, 1)
                        r, o = v_region(t)
                        act.wait_ge(v_ready, c * TPC + (t + 1))
                        nc.scalar.copy(xt_h[:, r, o:o + HID], w).then_inc(vh_ready, 1)
                    g_bank = [bank_u[0], bank_g[1], bank_u[1], bank_g[0]]

                    def gate(h):
                        act.wait_ge(gate_psum, c * HT + (h + 1))
                        nc.scalar.activation(gate_t[:, h, :], g_bank[h][:, :], ACT.Silu, bias=bias_g[:, h:h + 1]).then_inc(gate_ready, 1)

                    gate(0)
                    gate(1)
                    for b in range(BPC):
                        act.wait_ge(sim_psum, c * 2 + (b + 1))
                        nc.scalar.activation(work[:, b, :], bank_t[b][:, :], ACT.Relu, scale=1.0 / SEQ).then_inc(relu_ready, 1)
                    for b in range(BPC):
                        act.wait_ge(sq_ready, c * 2 + (b + 1))
                        nc.scalar.copy(mid_h[:, 1, b, :], work[:, b, :]).then_inc(ah_ready, 1)
                    gate(2)
                    gate(3)
                    x_high(c + (CHUNKS + 1), 0)
                    for n in range(4):
                        r, o = gated_region(2 * (n % 2), n // 2)
                        act.wait_ge(og_ready, c * 4 + (n + 1))
                        nc.scalar.copy(xt_h[:, r, o:o + CHUNK], work[:, 2 + n, :]).then_inc(oh_ready, 1)

            ffn(0)
            attention()
            ffn(1)

        @block.gpsimd
        def _(pool):
            nc.gpsimd.memset(ident[:, :], 0.0).then_inc(pool_step, 1)
            pool.wait_ge(pool_step, 1)
            nc.gpsimd.affine_select(out=ident[:, :], in_=ident[:, :], compare_op=ALU.not_equal, fill=1.0, base=0,
                                    pattern=[[-1, P]], channel_multiplier=1).then_inc(ident_ready, 1)

            def low(dst, src, high):
                return nc.gpsimd.tensor_tensor(dst, src, high.bitcast(F32), ALU.subtract)

            def split_low(s, par, n):
                pool.wait_ge(wh_ready, n)
                gu = w_raw_gu[:, s] if isinstance(s, int) else w_raw_gu[:, bass.ds(s, 1)].rearrange("p o k n -> p (o k) n")
                dn = w_raw_d[:, s] if isinstance(s, int) else w_raw_d[:, bass.ds(s, 1)].rearrange("p o k n -> p (o k) n")
                low(w_gu_l[:, par], gu, w_gu_h[:, par])
                low(w_d_l[:, par], dn, w_d_h[:, par]).then_inc(wl_ready, 1)

            def unit(layer, u, c, f):
                pool.wait_ge(mh_ready, n_uf(layer, u, f))
                low(mid_l[:, c % 2, f, :], work[:, 2 + f, :], mid_h[:, c % 2, f, :]).then_inc(ml_ready, 1)

            def ffn(layer):
                if layer == 0:
                    split_low(0, 0, 1)
                for u in range(2 * CHUNKS):
                    c = u % CHUNKS
                    unit(layer, u, c, 0)
                    unit(layer, u, c, 1)
                    if u in (1, CHUNKS + 1):
                        s = u // CHUNKS + 1
                        split_low(s, s % 2, layer * E + s + 1)
                with pool.Fori(1, E // 2 - 1) as pair:
                    for j in range(2 * CHUNKS):
                        c = j % CHUNKS
                        u = pair * (2 * CHUNKS) + j
                        unit(layer, u, c, 0)
                        unit(layer, u, c, 1)
                        if c == 1:
                            s = pair * 2 + (j // CHUNKS + 1)
                            split_low(s, (j // CHUNKS + 1) % 2, s + (layer * E + 1))
                for u in range(UNITS - 2 * CHUNKS, UNITS):
                    c, s = u % CHUNKS, u // CHUNKS + 1
                    unit(layer, u, c, 0)
                    unit(layer, u, c, 1)
                    if c == 1 and (s < E or layer == 0):
                        split_low(s % E, s % 2, layer * E + s + 1)
                    if layer == 0 and u == UNITS - 2 * CHUNKS:
                        pool.wait_ge(attn_wh_ready, 1)
                        low(w_hid_l[:, 0, :], w_hid_raw[:, 0, :], w_hid_h[:, 0, :])
                    if layer == 0 and u == UNITS - CHUNKS - 2:
                        low(w_hid_l[:, 1, :], w_hid_raw[:, 1, :], w_hid_h[:, 1, :])
                    if layer == 0 and u == UNITS - CHUNKS - 1:
                        low(w_out_l[:, :, :], w_out_raw, w_out_h[:, :, :])
                        low(w_qk_l[:, :, :], w_qk_raw[:, :, :], w_qk_h[:, :, :]).then_inc(attn_wl_ready, 1)

            def attention():
                with pool.Fori(0, CHUNKS) as c:
                    for i in range(2):
                        pool.wait_ge(qkh_ready, c * 2 + (i + 1))
                        low(mid_l[:, 0, i, :], work[:, 1 + i, :], mid_h[:, 0, i, :]).then_inc(qkl_ready, 1)
                    for t in range(TPC):
                        r, o = v_region(t)
                        pool.wait_ge(vh_ready, c * TPC + (t + 1))
                        low(xt_l[:, r, o:o + HID], work[:, 3 + t % 3, :], xt_h[:, r, o:o + HID]).then_inc(vl_ready, 1)
                    rows = x_res[:, bass.ds(c * TPC, TPC), :]
                    pool.wait_ge(resid_ready, c + 1)
                    pool.wait_ge(attn_loaded, N_ATTN_LOADS)
                    nc.gpsimd.tensor_tensor(rows, rows, bias_o[:, :].unsqueeze(1).to_broadcast([P, TPC, D]), ALU.add).then_inc(bias_added, 1)
                    for b in range(BPC):
                        pool.wait_ge(ah_ready, c * 2 + (b + 1))
                        low(mid_l[:, 1, b, :], work[:, b, :], mid_h[:, 1, b, :]).then_inc(al_ready, 1)
                    for n in range(4):
                        r, o = gated_region(2 * (n % 2), n // 2)
                        pool.wait_ge(oh_ready, c * 4 + (n + 1))
                        low(xt_l[:, r, o:o + CHUNK], work[:, 2 + n, :], xt_h[:, r, o:o + CHUNK]).then_inc(ol_ready, 1)

            ffn(0)
            attention()
            ffn(1)

        @block.vector
        def _(dve):
            step = [0, 0]

            def signal(ins):
                step[1] += 1
                ins.then_inc(dve_step, 1)
                return step[1]

            def after(n):
                dve.wait_ge(dve_step, step[0] + n)

            def in_turn(*chains, rounds=None):
                live = list(chains)
                while live and rounds != 0:
                    live = [x for x in live if next(x, True) is None]
                    rounds = rounds - 1 if rounds else None

            def layernorm(g, tile):
                v, y, a, b, scale, shift = (nw[:, i] for i in range(6))
                for t in range(TPC):
                    last = nc.vector.bn_stats(bn6[:, t, :], tile(t))
                n = signal(last)
                yield
                after(n)
                nc.vector.tensor_tensor(mv[:, :, 0:2], bn6[:, :, 1:3], bn6[:, :, 4:6], ALU.add)
                n = signal(nc.vector.tensor_tensor(a, bn6[:, :, 1], bn6[:, :, 4], ALU.subtract))
                yield
                after(n)
                nc.vector.scalar_tensor_tensor(out=b, in0=a, scalar=0.25, in1=a, op0=ALU.mult, op1=ALU.mult)
                nc.vector.tensor_scalar(v, mv[:, :, 1], 1.0 / D, EPS, ALU.mult, ALU.add)
                n = signal(nc.vector.tensor_scalar(mv[:, :, 0], mv[:, :, 0], 0.5, None, ALU.mult))
                yield
                after(n)
                n = signal(nc.vector.tensor_tensor(v, v, b, ALU.add))
                yield
                after(n)
                n = signal(nc.vector.tensor_scalar(a.bitcast(I32), v.bitcast(I32), 1, None, ALU.logical_shift_right))
                yield
                after(n)
                n = signal(nc.vector.tensor_scalar(y.bitcast(I32), a.bitcast(I32), -1.0, float(0x5f3759df), ALU.mult, ALU.add))
                yield
                for _ in range(3):
                    after(n)
                    n = signal(nc.vector.tensor_tensor(a, y, y, ALU.mult))
                    yield
                    after(n)
                    n = signal(nc.vector.scalar_tensor_tensor(out=b, in0=a, scalar=-0.5, in1=v, op0=ALU.mult, op1=ALU.mult))
                    yield
                    after(n)
                    n = signal(nc.vector.scalar_tensor_tensor(out=y, in0=b, scalar=1.5, in1=y, op0=ALU.add, op1=ALU.mult))
                    yield
                after(n)
                if not (isinstance(g, int) and g == 0):
                    dve.wait_ge(xt_psum, g)
                for t in range(TPC):
                    last = nc.vector.tensor_scalar(xn[:, t, :], tile(t), mv[:, t, 0:1], y[:, t:t + 1], ALU.subtract, ALU.mult)
                last.then_inc(xn_ready, 1)
                nc.vector.tensor_scalar(scale, y, 1.0, None, ALU.add)
                signal(nc.vector.scalar_tensor_tensor(out=shift, in0=mv[:, :, 0], scalar=-1.0, in1=y, op0=ALU.mult, op1=ALU.mult))

            def x_low(g, region):
                dve.wait_ge(xh_ready, g + 1)
                for k in range(KD):
                    o = slice(k * CHUNK, (k + 1) * CHUNK)
                    last = nc.vector.tensor_tensor(xt_l[:, region, o], bank_t[k][:, :], xt_h[:, region, o].bitcast(F32), ALU.subtract)
                last.then_inc(xl_ready, 1)

            def mid(layer, u, f):
                dve.wait_ge(silu_ready, n_uf(layer, u, f))
                if not (layer == 0 and isinstance(u, int) and u == 0):
                    dve.wait_ge(ml_ready, n_uf(layer, u, f) - KF)
                nc.vector.tensor_tensor(work[:, 2 + f, :], work[:, f, :], bank_u[f][:, :], ALU.mult).then_inc(mid_ready, 1)

            def add_down(layer, u, c, weight):
                for b in range(2):
                    dve.wait_ge(down_psum, n_down(layer, u, b))
                    if not isinstance(u, int) or u >= CHUNKS:
                        dve.wait_ge(added, n_added(layer, u, b) - 2 * CHUNKS)
                    for t in (2 * b, 2 * b + 1):
                        rows = x_res[:, c * TPC + t, :]
                        last = nc.vector.scalar_tensor_tensor(out=rows, in0=bank_d[b][:, (t % 2) * D:(t % 2 + 1) * D],
                                                              scalar=weight(c * TPC + t), in1=rows, op0=ALU.mult, op1=ALU.add)
                    last.then_inc(added, 1)

            def read_logits(layer, c):
                dve.wait_ge(logits_psum, layer * CHUNKS + c + 1)
                halves = bank_t[0][:, 0:TPC * 2 * E].rearrange("p (t a e) -> p t e a", t=TPC, a=2)
                nc.vector.tensor_reduce(rt[:, 0], halves, axis=AX.X, op=ALU.add).then_inc(logits_read, 1)

            def router_distance(layer, c):
                dve.wait_ge(tanh_z, layer * CHUNKS + c + 1)
                inh, d, diff = rt[:, 2], rt[:, 3], rt[:, 6]
                after(signal(nc.vector.tensor_scalar(inh, rt[:, 1], 0.5, 0.5, ALU.mult, ALU.add)))
                after(signal(nc.vector.tensor_scalar(diff, inh, GOLDEN_CENTER, None, ALU.subtract)))
                nc.vector.scalar_tensor_tensor(out=d, in0=diff, scalar=-1.0, in1=diff, op0=ALU.mult, op1=ALU.max).then_inc(dist_ready, 1)

            def router_weights(layer, c):
                inh, both = rt[:, 2], rt[:, 4:6]
                w, fb = rt[:, 4], rt[:, 5]
                upper, zone, rest = rt[:, 7], rt[:, 8], rt[:, 9]
                total, none = rs[:, 0], rs[:, 1]

                def per_token(v):
                    return v.unsqueeze(2).to_broadcast([P, TPC, E])

                nc.vector.tensor_scalar(upper, inh, GOLDEN_UPPER, None, ALU.is_le)
                dve.wait_ge(tanh_d, layer * CHUNKS + c + 1)
                n = signal(nc.vector.tensor_scalar(both, both, 1.0, None, ALU.add))
                yield
                after(n)
                nc.vector.scalar_tensor_tensor(out=zone, in0=inh, scalar=GOLDEN_LOWER, in1=upper, op0=ALU.is_ge, op1=ALU.mult)
                n = signal(nc.vector.reciprocal(both, both))
                yield
                after(n)
                n = signal(nc.vector.tensor_scalar(both, both, 2.0, -1.0, ALU.mult, ALU.add))
                yield
                after(n)
                nc.vector.tensor_tensor(w, w, zone, ALU.mult)
                for t in range(TPC):
                    last = nc.vector.max(top8[:, t, :], fb[:, t, :])
                n = signal(last)
                yield
                after(n)
                nc.vector.memset(top8[:, :, 2:8], -7.0)
                n = signal(nc.vector.tensor_reduce(total, w, axis=AX.X, op=ALU.add))
                yield
                after(n)
                for t in range(TPC):
                    last = nc.vector.match_replace(out=rest[:, t, :], in_to_replace=top8[:, t, :], in_values=fb[:, t, :], imm_value=-1.0)
                n = signal(last)
                nc.vector.tensor_scalar(none, total, 1e-8, None, ALU.is_lt)
                yield
                after(n)
                n = signal(nc.vector.scalar_tensor_tensor(out=fb, in0=rest, scalar=0.0, in1=fb, op0=ALU.is_lt, op1=ALU.mult))
                yield
                after(n)
                n = signal(nc.vector.tensor_tensor(fb, fb, per_token(none), ALU.mult))
                yield
                after(n)
                n = signal(nc.vector.tensor_tensor(w, w, fb, ALU.add))
                yield
                after(n)
                n = signal(nc.vector.tensor_reduce(total, w, axis=AX.X, op=ALU.add))
                yield
                after(n)
                n = signal(nc.vector.tensor_scalar(total, total, 1e-8, 2.0, ALU.max, ALU.mult))
                yield
                after(n)
                n = signal(nc.vector.reciprocal(total, total))
                yield
                after(n)
                signal(nc.vector.tensor_tensor(route[:, c * TPC:(c + 1) * TPC, :], w, per_token(total), ALU.mult))

            def low_rank(n):
                i, e = n // NL, n % NL
                s = E - NL + e
                dst = w_raw_d[:, s] if i == 2 else w_raw_gu[:, s, :, i * F:(i + 1) * F]
                dve.wait_ge(lora_psum, n + 1)
                nc.vector.tensor_tensor(dst, dst, bank_t[n % 2][:, :].rearrange("p (k n) -> p k n", k=2), ALU.add).then_inc(lora_added, 1)

            def ffn(layer):
                def tile(c):
                    return lambda t: x_res[:, c * TPC + t, :]

                if layer == 0:
                    dve.wait_ge(x_loaded[0], 16)
                    in_turn(layernorm(0, tile(0)))
                    dve.wait_ge(router_loaded, 32)
                    nc.vector.tensor_copy(wr_hl[:, :, 0, :], wr_raw[:, :, :])
                    after(signal(nc.vector.reciprocal(half_inv_temp[:, :], temp[:, :])))
                    after(signal(nc.vector.tensor_scalar(half_inv_temp[:, :], half_inv_temp[:, :], 0.5, None, ALU.mult)))
                    nc.vector.tensor_tensor(wr_hl[:, :, 1, :], wr_raw[:, :, :], wr_hl[:, :, 0, :].bitcast(F32), ALU.subtract).then_inc(router_w_ready, 1)
                    x_low(0, 0)
                for u in range(2 * CHUNKS):
                    c = u % CHUNKS
                    chains = []
                    if u + 1 < CHUNKS:
                        if layer == 0:
                            dve.wait_ge(x_loaded[u + 1], 16)
                        else:
                            dve.wait_ge(added, L_ADDED[1])
                        chains.append(layernorm(g_of(layer, u + 1), tile(u + 1)))
                    if 0 < u <= CHUNKS:
                        chains.append(router_weights(layer, u - 1))
                    in_turn(*chains)
                    mid(layer, u, 0)
                    if u < CHUNKS:
                        read_logits(layer, c)
                        router_distance(layer, c)
                    mid(layer, u, 1)
                    if u + 1 < CHUNKS:
                        x_low(g_of(layer, u + 1), u + 1)
                    if u > 0:
                        e = SLOT_EXPERT[(u - 1) // CHUNKS]
                        add_down(layer, u - 1, (u - 1) % CHUNKS, lambda n: route[:, n, e:e + 1])
                    if layer == 0 and u in (CHUNKS, CHUNKS + 1, CHUNKS + 2):
                        dve.wait_ge(slot_loaded[2], N_SLOT_LOADS * (E - 2))
                        low_rank(2 * (u - CHUNKS))
                        low_rank(2 * (u - CHUNKS) + 1)
                with dve.Fori(1, E // 2 - 1) as pair:
                    for j in range(2 * CHUNKS):
                        u = pair * (2 * CHUNKS) + j
                        mid(layer, u, 0)
                        mid(layer, u, 1)
                        e = pair * 2 + ((j - 1) // CHUNKS + NL)
                        add_down(layer, u - 1, (j - 1) % CHUNKS, lambda n: route[:, n, bass.ds(e, 1)])
                for u in range(UNITS - 2 * CHUNKS, UNITS):
                    if layer == 0 and u == UNITS - 2:
                        dve.wait_ge(added, n_added(layer, UNITS - CHUNKS, 1))
                        in_turn(layernorm(CHUNKS, tile(0)))
                    mid(layer, u, 0)
                    mid(layer, u, 1)
                    if layer == 0 and u == UNITS - 1:
                        x_low(CHUNKS, 0)
                    e = SLOT_EXPERT[(u - 1) // CHUNKS]
                    add_down(layer, u - 1, (u - 1) % CHUNKS, lambda n: route[:, n, e:e + 1])
                e = SLOT_EXPERT[E - 1]
                add_down(layer, UNITS - 1, CHUNKS - 1, lambda n: route[:, n, e:e + 1])

            def attention():
                before = step[1]
                with dve.Fori(0, CHUNKS) as c:
                    step[0], step[1] = c * LN_STEPS, before
                    v_bank = [bank_u[0], bank_g[1], bank_u[1], bank_g[0]]
                    av_bank = v_bank

                    def tile(chunk):
                        return lambda t: x_res[:, bass.ds(chunk * TPC + t, 1), :].rearrange("p o d -> p (o d)")

                    def values():
                        for t in range(TPC):
                            dve.wait_ge(v_psum, c * TPC + (t + 1))
                            if t == 3:
                                dve.wait_ge(vl_ready, c * TPC + 1)
                            nc.vector.tensor_tensor(work[:, 3 + t % 3, :], v_bank[t][:, :], bias_v[:, :], ALU.add).then_inc(vb_ready, 1)
                            yield
                            yield
                            yield
                            yield

                    after(before)
                    dve.wait_ge(added, c * 2 + A_ADDED)
                    for t in range(TPC):
                        last = nc.vector.tensor_scalar(tile(c)(t), tile(c)(t), nw[:, 4, t:t + 1], nw[:, 5, t:t + 1], ALU.mult, ALU.add)
                    last.then_inc(resid_ready, 1)
                    dve.wait_ge(qk_ready, c + 1)
                    for i in range(2):
                        nc.vector.tensor_scalar(work[:, 1 + i, :], work[:, 0, :], vecs[:, 1 + 2 * i:2 + 2 * i],
                                                vecs[:, 2 + 2 * i:3 + 2 * i], ALU.mult, ALU.add).then_inc(q_k_ready, 1)
                    in_turn(values(), layernorm(c + (CHUNKS + 1), tile((c + 1) % CHUNKS)))
                    assert step[1] - before == LN_STEPS
                    for b in range(BPC):
                        dve.wait_ge(relu_ready, c * 2 + (b + 1))
                        nc.vector.tensor_tensor(work[:, b, :], work[:, b, :], work[:, b, :], ALU.mult).then_inc(sq_ready, 1)
                    x_low(c + (CHUNKS + 1), 0)
                    for n in range(4):
                        b, hp = n // 2, n % 2
                        dve.wait_ge(av_psum, c * 4 + (n + 1))
                        nc.vector.tensor_tensor(work[:, 2 + n, :].rearrange("p (h i) -> p h i", h=2),
                                                av_bank[n][:, :].rearrange("p (h i) -> p h i", h=2),
                                                gate_t[:, 2 * hp:2 * hp + 2, b * SEQ:(b + 1) * SEQ], ALU.mult).then_inc(og_ready, 1)
                    dve.wait_ge(bias_added, c + 1)
                    for b in range(BPC):
                        dve.wait_ge(down_psum_attn, c * 2 + (b + 1))
                        rows = x_res[:, bass.ds(c * TPC + 2 * b, 2), :]
                        nc.vector.tensor_tensor(rows, bank_d[b][:, :].rearrange("p (t d) -> p t d", t=2), rows, ALU.add).then_inc(added, 1)
                step[0], step[1] = 0, before + CHUNKS * LN_STEPS

            LN_STEPS = 6 + 9 + 1
            ffn(0)
            attention()
            ffn(1)


_INS = ['L0_attn_x', 'L0_attn_W_hidden', 'L0_attn_b_hidden', 'L0_attn_W_qk', 'L0_attn_b_qk', 'L0_attn_gamma_q',
        'L0_attn_beta_q', 'L0_attn_gamma_k', 'L0_attn_beta_k', 'L0_attn_W_out', 'L0_attn_b_out', 'L0_ffn_Wg',
        'L0_ffn_Wu', 'L0_ffn_Wd', 'L0_ffn_Ga', 'L0_ffn_Gb', 'L0_ffn_Ua', 'L0_ffn_Ub', 'L0_ffn_Da', 'L0_ffn_Db',
        'L0_ffn_Wr', 'L0_ffn_temperature']


def kernel(**inputs):
    import numpy as _np
    import concourse.bacc as _bacc
    from concourse.bass_utils import run_bass_kernel_spmd as _run

    nc = _bacc.Bacc("TRN2", target_bir_lowering=False, num_devices=1)
    arrays, args = {}, []
    for name in _INS:
        a = _np.ascontiguousarray(inputs[name])
        arrays[f"in_{name}"] = a
        args.append(nc.dram_tensor(f"in_{name}", a.shape, F32, kind="ExternalInput").ap())
    args.append(nc.dram_tensor("out_x", (SEQS, SEQ, D), F32, kind="ExternalOutput").ap())
    build(nc, *args)
    r = _run(nc, [arrays], core_ids=[0])
    return r.results[0]["out_x"]
```
